# Optimizing a Trainium2 kernel written in Bass

```python
import numpy as np
import jax
import jax.numpy as jnp

def _softmax(x, axis=-1):
    return jax.nn.softmax(x, axis=axis)

def _gelu(x):
    return jax.nn.gelu(x, approximate=True)

def _silu(x):
    return jax.nn.silu(x)

def _sigmoid(x):
    return jax.nn.sigmoid(x)

def _layernorm(x, axis=-1, eps=1e-05):
    m = jnp.mean(x, axis=axis, keepdims=True)
    v = jnp.var(x, axis=axis, keepdims=True)
    return (x - m) / jnp.sqrt(v + eps)

def _scatter_add(tgt, idx, src, axis=0):
    return tgt.at[idx].add(src)

def _segment_sum(src, seg, n):
    return jax.ops.segment_sum(src, seg, n)
kernel_name = 'mk_gnn_preln_d4_gnn_r16_af5de2'

def setup_inputs(seed: int=0):
    np.random.seed(seed)
    _w = jnp.asarray

    def _rec_inputs():
        import jax
        import jax.numpy as jnp
        _gk = jax.random.key(seed)
        x = -0.0002117 + 1 * jax.random.normal(jax.random.fold_in(_gk, 1), (3125, 512), jnp.float32)
        _s = jax.random.randint(jax.random.fold_in(_gk, 2), (25000,), 0, 3125, jnp.int32)
        _d = jax.random.randint(jax.random.fold_in(_gk, 3), (25000,), 0, 3125, jnp.int32)
        _loop = jnp.arange(3125, dtype=jnp.int32)
        src = jnp.concatenate([_s, _d, _loop])
        dst = jnp.concatenate([_d, _s, _loop])
        _o = jnp.argsort(dst, stable=True)
        src = src[_o]
        dst = dst[_o]
        edge_weight = jax.random.uniform(jax.random.fold_in(_gk, 13), (53125,), jnp.float32, 0.0, 0.999998)
        return (x, src, dst, edge_weight)
    x, src, dst, edge_weight = _rec_inputs()

    def _L0_gnn_setup():
        import jax, jax.numpy as jnp
        import numpy as np
        N_NODES = 3125
        N_EDGES = 50000
        M_IN = 512
        H_OUT = 512
        key = jax.random.key(seed)
        k1, k2, k3, k4, k5 = jax.random.split(key, 5)
        X = jax.random.normal(k1, (N_NODES, M_IN), dtype=jnp.float32)
        limit = float(np.sqrt(6.0 / (M_IN + H_OUT)))
        W = jax.random.uniform(k2, (M_IN, H_OUT), dtype=jnp.float32, minval=-limit, maxval=limit)
        edge_src = jax.random.randint(k3, (N_EDGES,), 0, N_NODES, dtype=jnp.int64 if jax.config.jax_enable_x64 else jnp.int32)
        edge_dst = jax.random.randint(k4, (N_EDGES,), 0, N_NODES, dtype=jnp.int64 if jax.config.jax_enable_x64 else jnp.int32)
        edge_vals = jax.random.uniform(k5, (N_EDGES,), dtype=jnp.float32, minval=0.0, maxval=1.0)
        return {'X': X, 'W': W, 'edge_src': edge_src, 'edge_dst': edge_dst, 'edge_vals': edge_vals}
    _L0_gnn_all = _L0_gnn_setup()
    _L0_gnn_in = {k: v for k, v in _L0_gnn_all.items() if k in ('W',)}
    del _L0_gnn_all

    def _L1_gnn_setup():
        import jax, jax.numpy as jnp
        import numpy as np
        N_NODES = 3125
        N_EDGES = 25000
        IN_DIM = 512
        OUT_DIM = 512
        key = jax.random.key(seed)
        k1, k2, k3, k4 = jax.random.split(key, 4)
        x = jax.random.normal(k1, (N_NODES, IN_DIM), dtype=jnp.float32)
        edge_index = jax.random.randint(k2, (2, N_EDGES), 0, N_NODES, dtype=jnp.int64)
        W = jax.random.normal(k3, (OUT_DIM, IN_DIM), dtype=jnp.float32) / np.sqrt(IN_DIM)
        b = jax.random.normal(k4, (OUT_DIM,), dtype=jnp.float32) * 0.01
        return {'x': x, 'edge_index': edge_index, 'W': W, 'b': b}
    _L1_gnn_all = _L1_gnn_setup()
    _L1_gnn_in = {k: v for k, v in _L1_gnn_all.items() if k in ('W', 'b')}
    del _L1_gnn_all

    def _L2_gnn_setup():
        import jax, jax.numpy as jnp
        import numpy as np
        N_NODES = 625
        N_EDGES = 10000
        D = 512
        key = jax.random.key(seed)
        k_h, k_e, k_w1, k_w2 = jax.random.split(key, 4)
        h = jax.random.normal(k_h, (N_NODES, D), dtype=jnp.float32)
        edge_index = jax.random.randint(k_e, (2, N_EDGES), 0, N_NODES, dtype=jnp.int64)
        scale = 1.0 / np.sqrt(D)
        W1 = jax.random.normal(k_w1, (D, D), dtype=jnp.float32) * scale
        b1 = jnp.zeros((D,), dtype=jnp.float32)
        W2 = jax.random.normal(k_w2, (D, D), dtype=jnp.float32) * scale
        b2 = jnp.zeros((D,), dtype=jnp.float32)
        return {'h': h, 'edge_index': edge_index, 'W1': W1, 'b1': b1, 'W2': W2, 'b2': b2}
    _L2_gnn_all = _L2_gnn_setup()
    _L2_gnn_in = {k: v for k, v in _L2_gnn_all.items() if k in ('W1', 'b1', 'W2', 'b2')}
    del _L2_gnn_all

    def _L3_gnn_setup():
        import jax, jax.numpy as jnp
        import numpy as np
        N, E, H, D_IN, D_PRIME = (3125, 50000, 8, 512, 64)

        def _segment_softmax(scores, seg, num_segments):
            smax = jax.ops.segment_max(scores, seg, num_segments=num_segments)
            ex = jnp.exp(scores - smax[seg])
            denom = jax.ops.segment_sum(ex, seg, num_segments=num_segments)
            return ex / denom[seg]
        key = jax.random.key(seed)
        ks = jax.random.split(key, 6)
        x = jax.random.normal(ks[0], (N, D_IN), dtype=jnp.float32)
        edge_index = jax.random.randint(ks[1], (2, E), 0, N)
        Ws = jax.random.normal(ks[2], (H, D_IN, D_PRIME), dtype=jnp.float32) * 0.05
        Wb = jax.random.normal(ks[3], (H, D_PRIME), dtype=jnp.float32) * 0.05
        a_w = jax.random.normal(ks[4], (H, 2 * D_PRIME), dtype=jnp.float32) * 0.05
        a_b = jax.random.normal(ks[5], (H,), dtype=jnp.float32) * 0.05
        return dict(x=x, edge_index=edge_index, Ws=Ws, Wb=Wb, a_w=a_w, a_b=a_b)
    _L3_gnn_all = _L3_gnn_setup()
    _L3_gnn_in = {k: v for k, v in _L3_gnn_all.items() if k in ('Ws', 'Wb', 'a_w', 'a_b')}
    del _L3_gnn_all
    return {'x': x, 'src': src, 'dst': dst, 'edge_weight': edge_weight, 'L0_gnn_W': _L0_gnn_in['W'], 'L1_gnn_W': _L1_gnn_in['W'], 'L1_gnn_b': _L1_gnn_in['b'], 'L2_gnn_W1': _L2_gnn_in['W1'], 'L2_gnn_b1': _L2_gnn_in['b1'], 'L2_gnn_W2': _L2_gnn_in['W2'], 'L2_gnn_b2': _L2_gnn_in['b2'], 'L3_gnn_Ws': _L3_gnn_in['Ws'], 'L3_gnn_Wb': _L3_gnn_in['Wb'], 'L3_gnn_a_w': _L3_gnn_in['a_w'], 'L3_gnn_a_b': _L3_gnn_in['a_b']}

def reference(x, src, dst, edge_weight, L0_gnn_W, L1_gnn_W, L1_gnn_b, L2_gnn_W1, L2_gnn_b1, L2_gnn_W2, L2_gnn_b2, L3_gnn_Ws, L3_gnn_Wb, L3_gnn_a_w, L3_gnn_a_b):
    import jax
    import jax.numpy as jnp

    def _L0_gnn_ref(X, W, edge_src, edge_dst, edge_vals):
        import jax, jax.numpy as jnp
        import numpy as np
        N_NODES = 3125
        N_EDGES = 50000
        M_IN = 512
        H_OUT = 512
        Z = jnp.matmul(X, W)
        msg = Z[edge_src] * edge_vals[:, None]
        agg = jax.ops.segment_sum(msg, edge_dst, num_segments=X.shape[0])
        return jax.nn.relu(agg)

    def _L1_gnn_ref(x, edge_index, W, b):
        import jax, jax.numpy as jnp
        import numpy as np
        N_NODES = 3125
        N_EDGES = 25000
        IN_DIM = 512
        OUT_DIM = 512
        n = x.shape[0]
        loops = jnp.arange(n, dtype=edge_index.dtype)
        row = jnp.concatenate([edge_index[0], loops])
        col = jnp.concatenate([edge_index[1], loops])
        deg = jax.ops.segment_sum(jnp.ones(row.shape[0], dtype=x.dtype), row, num_segments=n)
        dis = jax.lax.rsqrt(deg)
        norm = dis[row] * dis[col]
        h = x @ W.T + b
        out = jax.ops.segment_sum(norm[:, None] * h[row], col, num_segments=n)
        return jax.nn.relu(out)

    def _L2_gnn_ref(h, edge_index, W1, b1, W2, b2):
        import jax, jax.numpy as jnp
        import numpy as np
        N_NODES = 625
        N_EDGES = 10000
        D = 512
        send, rec = (edge_index[0], edge_index[1])
        agg = jax.ops.segment_sum(h[send], rec, num_segments=h.shape[0])
        x = h + agg
        x = jax.nn.relu(x @ W1 + b1)
        x = x @ W2 + b2
        return x

    def _L3_gnn_ref(x, edge_index, Ws, Wb, a_w, a_b):
        import jax, jax.numpy as jnp
        import numpy as np
        N, E, H, D_IN, D_PRIME = (3125, 50000, 8, 512, 64)

        def _segment_softmax(scores, seg, num_segments):
            smax = jax.ops.segment_max(scores, seg, num_segments=num_segments)
            ex = jnp.exp(scores - smax[seg])
            denom = jax.ops.segment_sum(ex, seg, num_segments=num_segments)
            return ex / denom[seg]
        v_src, v_tgt = (edge_index[0], edge_index[1])
        n = x.shape[0]
        outs = []
        for h in range(Ws.shape[0]):
            Wx = x @ Ws[h] + Wb[h]
            d = Wx.shape[-1]
            s = Wx[v_tgt] @ a_w[h, :d] + Wx[v_src] @ a_w[h, d:] + a_b[h]
            s = jax.nn.leaky_relu(s, negative_slope=0.2)
            alpha = _segment_softmax(s, v_tgt, n)
            outs.append(jax.ops.segment_sum(alpha[:, None] * Wx[v_src], v_tgt, num_segments=n))
        return jnp.stack(outs, axis=1).reshape(n, -1)
    edge_index = jnp.stack([src, dst])
    h = jnp.maximum(_layernorm(x, axis=-1), 0.0)
    x = x + _L0_gnn_ref(h, L0_gnn_W, src, dst, edge_weight)
    h = jnp.maximum(_layernorm(x, axis=-1), 0.0)
    x = x + _L1_gnn_ref(h, edge_index, L1_gnn_W, L1_gnn_b)
    h = jnp.maximum(_layernorm(x, axis=-1), 0.0)
    x = x + _L2_gnn_ref(h, edge_index, L2_gnn_W1, L2_gnn_b1, L2_gnn_W2, L2_gnn_b2)
    h = jnp.maximum(_layernorm(x, axis=-1), 0.0)
    x = x + _L3_gnn_ref(h, edge_index, L3_gnn_Ws, L3_gnn_Wb, L3_gnn_a_w, L3_gnn_a_b)
    return x

_drawn_inputs = setup_inputs


def setup_inputs(seed=0):
    import zlib

    import numpy as np

    out = dict(_drawn_inputs(seed))
    spreads = {'L2_gnn_b1': (0.0, 0.8), 'L2_gnn_b2': (0.0, 0.8)}
    factors = {'L1_gnn_b': 24.857, 'L3_gnn_Wb': 8.0, 'L3_gnn_a_w': 64.0, 'L3_gnn_a_b': 64.0}
    for name, (base, spread) in spreads.items():
        noise = np.random.default_rng([zlib.crc32(name.encode()), seed]).standard_normal(out[name].shape)
        drawn = base * np.exp(spread * noise) if base else spread * noise
        out[name] = jnp.asarray(drawn.astype(out[name].dtype))
    for name, factor in factors.items():
        out[name] = (out[name] * factor).astype(out[name].dtype)
    return out
```

```python
import numpy as np
import concourse.bass as bass
from concourse import mybir
from contextlib import ExitStack

F32 = mybir.dt.float32
I32 = mybir.dt.int32
BF16 = mybir.dt.bfloat16
ALU = mybir.AluOpType
ACT = mybir.ActivationFunctionType
AX = mybir.AxisListType


class Count:

    def __init__(self, sem):
        self.sem, self.value = sem, 0

    def after(self, instruction, by=1):
        instruction.then_inc(self.sem, by)
        self.value += by
        return (self.sem, self.value)


def build(nc, x_in, src_in, dst_in, w_in, W0_in, W1_in, b1_in, G1_in, g1_in, G2_in, g2_in,
          Ws_in, Wb_in, aw_in, ab_in, out):
    N, D = x_in.shape
    E = src_in.shape[0]
    H, _, DP = Ws_in.shape
    TN = 125
    TILES = N // TN
    CE = 128
    CHUNKS = -(-E // CE)
    STEPS = CHUNKS + TILES - 1
    RB = 4
    RS = STEPS // RB
    KB = D // 128
    EC = 4
    EP = CHUNKS // EC
    EROW = EC * CE
    RING = 16
    SELS = 8
    AHEAD = 4
    NAGG = 4
    EPS = 1e-5
    BIG = 1e30
    FAR = 1 << 20
    assert TILES * TN == N and RB * RS == STEPS and EP * EC == CHUNKS and KB * 128 == D and H * DP == D

    ctx = ExitStack()
    with ctx:
        def sb(name, shape, dt=F32):
            return ctx.enter_context(nc.sbuf_tensor(name, shape, dt))

        def count(name):
            return Count(ctx.enter_context(nc.semaphore(name)))

        V, A, P, G, S = nc.vector, nc.scalar, nc.tensor, nc.gpsimd, nc.sync

        def wait(engine, *marks):
            for mark in marks:
                if mark is not None:
                    engine.wait_ge(*mark)

        edge_rows = nc.dram_tensor("edge_rows", (CHUNKS, 3 * CE), I32, kind="Internal").ap()
        table = [nc.dram_tensor(f"table{n}", (N, D), F32, kind="Internal").ap() for n in range(4)]
        score_table = nc.dram_tensor("score_table", (N, H), F32, kind="Internal").ap()

        x = sb("x", [TN, TILES, D])
        acc = sb("acc", [TN, TILES, D])
        ring = sb("ring", [CE, RING, D])
        sel = sb("sel", [CE, SELS, TN])
        wbuf = sb("wbuf", [128, KB, D])
        ident = sb("ident", [128, 128])
        node_iota = sb("node_iota", [128, TN])
        ones = sb("ones", [128, 128])
        eps = sb("eps", [128, 1])
        src_t = sb("src_t", [CE, STEPS], I32)
        dl_t = sb("dl_t", [CE, STEPS])
        w_t = sb("w_t", [CE, STEPS])
        tile_row = sb("tile_row", [1, STEPS], I32)
        dstf = sb("dstf", [RS, RB, CE])
        valid = sb("valid", [RS, RB, CE])
        dis = sb("dis", [TN, TILES])
        stats = sb("stats", [TN, 2, 6])
        mv = sb("mv", [TN, 2, 2])
        rstd = sb("rstd", [TN, 2, 2])
        hbuf = sb("hbuf", [TN, 2, D])
        hT = sb("hT", [128, 2, KB, TN])
        zbuf = sb("zbuf", [TN, 3, D])
        bias_bc = sb("bias_bc", [TN, D])
        wa = sb("wa", [128, KB, 2 * H])
        scb = sb("scb", [TN, 2, 2 * H])
        sc_bias = sb("sc_bias", [TN, 2 * H])
        t_all = sb("t_all", [TN, TILES, H])
        g1col = sb("g1col", [128, KB])

        bank = [ctx.enter_context(nc.psum_tensor(f"bank{n}", [128, 512], F32)) for n in range(8)]

        c_const = count("c_const")
        c_v = count("c_v")
        c_a = count("c_a")
        c_p = count("c_p")
        c_g = count("c_g")
        c_ld = count("c_ld")
        c_lx = count("c_lx")
        c_er = count("c_er")
        c_pt = count("c_pt")
        c_w = count("c_w")
        c_st = [count(f"c_st{n}") for n in range(3)]
        c_ring = [count(f"c_ring{n}") for n in range(RING)]
        c_gl = count("c_gl")
        c_out = count("c_out")

        m = c_g.after(G.memset(ident[:, :], 0.0))
        wait(G, m)
        k_ident = c_g.after(G.affine_select(out=ident[:, :], in_=ident[:, :], compare_op=ALU.not_equal,
                                            fill=1.0, base=0, pattern=[[-1, 128]], channel_multiplier=1))
        iota_i = sb("iota_i", [128, 128], I32)
        m = c_g.after(G.iota(iota_i[:, 0:TN], pattern=[[1, TN]], base=0, channel_multiplier=0))
        wait(V, m)
        k_iota = c_v.after(V.tensor_copy(node_iota[:, :], iota_i[:, 0:TN]))
        step_i = sb("step_i", [RS, RB], I32)
        step_f = sb("step_f", [RS, RB])
        m = c_g.after(G.iota(step_i[:, :], pattern=[[RS, RB]], base=0, channel_multiplier=1))
        wait(V, m)
        c_v.after(V.tensor_copy(step_f[:, :], step_i[:, :]))
        tile_i = sb("tile_i", [128, TILES - 1], I32)
        tile_f = sb("tile_f", [128, TILES - 1])
        m = c_g.after(G.iota(tile_i[:, :], pattern=[[CE, TILES - 1]], base=CE, channel_multiplier=0))
        wait(V, m)
        c_v.after(V.tensor_copy(tile_f[:, :], tile_i[:, :]))
        c_v.after(V.memset(ones[:, :], 1.0))
        k_const = c_v.after(V.memset(eps[:, :], EPS))

        ed = ring[0:EP, 0:3, :].rearrange("p a b -> p (a b)").bitcast(I32).rearrange(
            "p (c a e) -> p c a e", c=EC, a=3)
        edf = ring[0:EP, 0:3, :].rearrange("p a b -> p (a b)").rearrange("p (c a e) -> p c a e", c=EC, a=3)
        for a, value in ((0, N + 2 * TN), (1, FAR), (2, 0)):
            k_pad = c_v.after(V.memset(ed[:, :, a, :], value))
        wait(S, k_pad)
        full = E // EROW
        rest = E - full * EROW
        rc = rest // CE
        for a, arr in enumerate((src_in, dst_in, w_in)):
            e = edf if a == 2 else ed
            k_ed = c_ld.after(S.dma_start(e[0:full, :, a, :], arr[0:full * EROW].rearrange(
                "(p c e) -> p c e", c=EC, e=CE)), 16)
            if rc:
                k_ed = c_ld.after(S.dma_start(e[full:full + 1, 0:rc, a, :], arr[full * EROW:full * EROW + rc * CE]
                                              .rearrange("(p c e) -> p c e", p=1, e=CE)), 16)
            if rest % CE:
                k_ed = c_ld.after(S.dma_start(e[full:full + 1, rc, a, 0:rest % CE],
                                              arr[full * EROW + rc * CE:E].rearrange("(p e) -> p e", p=1)), 16)
        wait(S, k_ed)
        k_er = c_er.after(S.dma_start(edge_rows.rearrange("(p c) e -> p (c e)", c=EC),
                                      ed.rearrange("p c a e -> p (c a e)")), 16)
        for q in range(5):
            n = TILES // 5
            k_x = c_lx.after(A.dma_start(x[:, q * n:(q + 1) * n, :],
                                         x_in[q * n * TN:(q + 1) * n * TN, :].rearrange("(t p) d -> p t d", p=TN)), 16)
        c_w.after(A.dma_start(wbuf[:, :, :], W0_in.rearrange("(k p) d -> p k d", p=128)), 16)
        k_w = (c_w.sem, c_w.value)

        df = ring[0:EP, 4, :]
        sf = ring[0:EP, 5, :]
        junk = ring[0:EP, 6, :]
        cnt = sb("cnt", [EP, TILES - 1])
        wait(V, k_ed)
        c_v.after(V.tensor_copy(df.rearrange("p (c e) -> p c e", c=EC), ed[:, :, 1, :]))
        m = c_v.after(V.tensor_copy(sf.rearrange("p (c e) -> p c e", c=EC), ed[:, :, 0, :]))
        wait(V, m)
        for t in range(1, TILES):
            m = c_v.after(V.tensor_scalar(out=junk, in0=df, scalar1=float(t * TN), scalar2=None, op0=ALU.is_lt,
                                          op1=ALU.add, accum_out=cnt[:, t - 1:t]))
            wait(V, m)
        wait(P, m)
        m = c_p.after(P.matmul(bank[0][:, 0:TILES - 1], ones[0:EP, :], cnt[:, :], start=True, stop=True))
        thr = sb("thr", [128, TILES - 1])
        lim = sb("lim", [RS, RB])
        tstep = sb("tstep", [RS, RB])
        tn_step = sb("tn_step", [RS, RB])
        gstep = sb("gstep", [RS, RB], I32)
        thr_junk = sb("thr_junk", [RS, TILES - 1])
        wait(V, m)
        c_v.after(V.tensor_tensor(thr[:, :], bank[0][:, 0:TILES - 1], tile_f[:, :], ALU.add))
        m = c_v.after(V.tensor_scalar(out=lim[:, :], in0=step_f[:, :], scalar1=1.0, scalar2=float(CE),
                                      op0=ALU.add, op1=ALU.mult))
        wait(V, m)
        for b in range(RB):
            m = c_v.after(V.tensor_scalar(out=thr_junk[:, :], in0=thr[0:RS, :], scalar1=lim[:, b:b + 1], scalar2=None,
                                          op0=ALU.is_lt, op1=ALU.add, accum_out=tstep[:, b:b + 1]))
            wait(V, m)
        c_v.after(V.tensor_scalar(out=tn_step[:, :], in0=tstep[:, :], scalar1=float(TN), scalar2=None, op0=ALU.mult))
        k_g = c_v.after(V.tensor_tensor(gstep[:, :], step_f[:, :], tstep[:, :], ALU.subtract))
        rows = [ring[0:RS, 8 + b, 0:3 * CE] for b in range(RB)]
        wait(G, k_g, k_er)
        for b in range(RB):
            k_pt = c_pt.after(G.indirect_dma_start(
                out=rows[b].bitcast(I32), out_offset=None, in_=edge_rows[:, :],
                in_offset=bass.IndirectOffsetOnAxis(ap=gstep[:, b:b + 1], axis=0)), 16)
        wait(V, k_pt, k_g)
        rsf = sb("rsf", [RS, RB, 2, CE])
        for b in range(RB):
            ri = rows[b].bitcast(I32)
            c_v.after(V.tensor_copy(rsf[:, b, 0, :], ri[:, 0:CE]))
            c_v.after(V.tensor_scalar(out=rsf[:, b, 1, :], in0=ri[:, CE:2 * CE], scalar1=tn_step[:, b:b + 1],
                                      scalar2=None, op0=ALU.subtract))
            m = c_v.after(V.tensor_copy(dstf[:, b, :], ri[:, CE:2 * CE]))
        wait(V, m)
        m = c_v.after(V.tensor_scalar(out=valid[:, :, :], in0=rsf[:, :, 1, :], scalar1=0.0, scalar2=None, op0=ALU.is_ge))
        wait(V, m)
        k_valid = c_v.after(V.scalar_tensor_tensor(out=valid[:, :, :], in0=rsf[:, :, 1, :], scalar=float(TN),
                                                   in1=valid[:, :, :], op0=ALU.is_lt, op1=ALU.mult))
        wait(P, m, k_ident, k_pt)
        for b in range(RB):
            for a in range(3):
                piece = rows[b][:, 2 * CE:3 * CE] if a == 2 else rsf[:, b, a, :]
                m = c_p.after(P.transpose(bank[a + 1][:, b * RS:(b + 1) * RS], piece, ident[0:RS, 0:RS]))
            m = c_p.after(P.transpose(bank[4][0:1, b * RS:(b + 1) * RS], tstep[:, b:b + 1], ident[0:RS, 0:RS]))
        wait(V, m)
        c_v.after(V.tensor_scalar(out=src_t[:, :], in0=bank[1][:, 0:STEPS], scalar1=float(N - 1), scalar2=None, op0=ALU.min))
        c_v.after(V.tensor_copy(dl_t[:, :], bank[2][:, 0:STEPS]))
        c_v.after(V.tensor_copy(w_t[:, :], bank[3][:, 0:STEPS]))
        k_tables = c_v.after(V.tensor_copy(tile_row[:, :], bank[4][0:1, 0:STEPS]))

        hi = ring[0:EP, 7, :]
        lo = ring[0:EP, 8, :]
        hi_hot = acc[0:EP, 0:7, :].rearrange("p a b -> p (a b)").bitcast(BF16)[:, 0:EROW * (TILES // 2 + 1)]
        HB = 8
        hot_lo = sb("hot_lo", [EP, 2, HB, TN], BF16)
        hot_hi = acc[0:EP, 0:13, :].rearrange("p a b -> p (a b)").bitcast(BF16)[:, 0:TILES * EROW].rearrange(
            "p (t e) -> p t e", t=TILES)
        wait(V, k_tables)
        m = c_v.after(V.tensor_scalar(out=hi, in0=sf, scalar1=float(TN), scalar2=None, op0=ALU.is_ge))
        for t in range(2, TILES + 2):
            wait(V, m)
            m = c_v.after(V.scalar_tensor_tensor(out=hi, in0=sf, scalar=float(t * TN), in1=hi, op0=ALU.is_ge, op1=ALU.add))
        wait(V, m)
        m = c_v.after(V.scalar_tensor_tensor(out=lo, in0=hi, scalar=float(-TN), in1=sf, op0=ALU.mult, op1=ALU.add))
        for t in range(TILES):
            m = c_v.after(V.tensor_scalar(out=hot_hi[:, t, :], in0=hi, scalar1=float(t), scalar2=None, op0=ALU.is_equal))
        wait(V, m)
        k_lo_free = [None, None]
        wait(P, m)
        for q in range(EROW // HB):
            wait(V, k_lo_free[q % 2])
            m = c_v.after(V.tensor_tensor(hot_lo[:, q % 2, :, :],
                                          node_iota[0:EP, None, :].to_broadcast([EP, HB, TN]),
                                          lo[:, q * HB:(q + 1) * HB, None].to_broadcast([EP, HB, TN]), ALU.is_equal))
            wait(P, m)
            for j in range(HB):
                e = q * HB + j
                last = P.matmul(bank[0][0:TN, 0:TILES], hot_lo[:, q % 2, j, :], hot_hi[:, :, e],
                                start=(e == 0), stop=(e == EROW - 1))
            k_lo_free[q % 2] = c_p.after(last)
        wait(V, k_lo_free[1])
        m = c_v.after(V.tensor_scalar(out=dis[:, :], in0=bank[0][0:TN, 0:TILES], scalar1=1.0, scalar2=None, op0=ALU.add))
        wait(A, m)
        m = c_a.after(A.activation(dis[:, :], dis[:, :], ACT.Sqrt))
        wait(V, m)
        k_dis = c_v.after(V.reciprocal(dis[:, :], dis[:, :]))

        free = {}

        def norm(t, before, dest, dest_free=None):
            q = t % 2
            wait(V, *before)
            wait(V, free.get(("mv", q)))
            m = c_v.after(V.bn_stats(stats[:, q, :], x[:, t, :]))
            wait(V, m)
            m = c_v.after(V.bn_aggr(mv[:, q, :], stats[:, q, :]))
            wait(A, m)
            m = c_a.after(A.activation(rstd[:, q, 0:1], mv[:, q, 1:2], ACT.Sqrt, bias=eps[0:TN, :]))
            wait(V, m)
            m = c_v.after(V.reciprocal(rstd[:, q, 0:1], rstd[:, q, 0:1]))
            wait(V, m)
            m = c_v.after(V.tensor_scalar(out=rstd[:, q, 1:2], in0=mv[:, q, 0:1], scalar1=-1.0,
                                          scalar2=rstd[:, q, 0:1], op0=ALU.mult, op1=ALU.mult))
            wait(A, m, dest_free)
            free["mv", q] = c_a.after(A.activation(dest, x[:, t, :], ACT.Relu, bias=rstd[:, q, 1:2], scale=rstd[:, q, 0:1]))
            return free["mv", q]

        def transposed(t, rows_ap, ready):
            q = t % 2
            wait(P, ready, free.get(("bankT", q)))
            for k in range(KB):
                last = P.transpose(bank[4 + q][:, k * TN:(k + 1) * TN], rows_ap[:, k * 128:(k + 1) * 128], ident[0:TN, 0:TN])
            read = c_p.after(last)
            wait(A, read, free.get(("hT", q)))
            free["bankT", q] = c_a.after(A.copy(hT[:, q, :, :].rearrange("p k n -> p (k n)"), bank[4 + q][:, 0:KB * TN]))
            return read, free["bankT", q]

        def project(t, ready, weight):
            q = t % 2
            wait(P, ready, free.get(("bankZ", q)))
            for k in range(KB):
                last = P.matmul(bank[6 + q][0:TN, :], hT[:, q, k, :], weight[:, k, :], start=(k == 0), stop=(k == KB - 1))
            return c_p.after(last)

        def store(t, dest, rows_ap, ready):
            wait(S, ready)
            return c_st[t % 3].after(S.dma_start(dest[t * TN:(t + 1) * TN, :], rows_ap), 16)

        done = {"pe": [], "acc": None}

        def aggregate(layer, target, weights, table_ready, target_ready, alpha=None):
            base = len(done["pe"])
            sels = {}
            wait(V, *target_ready)

            def select(i):
                n = base + i
                if n >= SELS:
                    wait(V, done["pe"][n - SELS])
                if weights:
                    ins = V.tensor_scalar(out=sel[:, n % SELS, :], in0=node_iota[:, :], scalar1=dl_t[:, i:i + 1],
                                          scalar2=w_t[:, i:i + 1], op0=ALU.is_equal, op1=ALU.mult)
                else:
                    ins = V.tensor_scalar(out=sel[:, n % SELS, :], in0=node_iota[:, :], scalar1=dl_t[:, i:i + 1],
                                          scalar2=None, op0=ALU.is_equal)
                sels[i] = c_v.after(ins)

            wait(G, *table_ready)
            acc_marks = {}
            gathered = {}
            for i in range(STEPS):
                n = base + i
                if n >= RING:
                    wait(G, done["pe"][n - RING])
                gathered[i] = None
                pass_slot = n % RING
                gathered[i] = c_ring[pass_slot].after(G.indirect_dma_start(
                    out=ring[:, pass_slot, :], out_offset=None, in_=table[layer][:, :],
                    in_offset=bass.IndirectOffsetOnAxis(ap=src_t[:, i:i + 1], axis=0)), 16)
                if i == 0:
                    for j in range(AHEAD):
                        select(j)
                if i + AHEAD < STEPS:
                    select(i + AHEAD)
                rows_ready = gathered[i]
                if alpha is not None:
                    wait(V, gathered[i])
                    slot = ring[:, pass_slot, :].rearrange("p (h j) -> p h j", h=H)
                    rows_ready = c_v.after(V.tensor_tensor(slot, slot,
                                                           alpha[:, i, :, None].to_broadcast([CE, H, DP]), ALU.mult))
                wait(P, rows_ready, sels[i], acc_marks.get(i - NAGG))
                mark = c_p.after(P.matmul(bank[n % NAGG][0:TN, :], sel[:, n % SELS, :], ring[:, pass_slot, :],
                                          start=True, stop=True))
                done["pe"].append(mark)
                t = V.value_load(tile_row[0:1, i:i + 1], min_val=0, max_val=TILES - 1)
                wait(V, mark, done["acc"])
                part = target[:, bass.ds(t, 1), :].rearrange("p a d -> p (a d)")
                done["acc"] = acc_marks[i] = c_v.after(V.tensor_tensor(part, part, bank[n % NAGG][0:TN, :], ALU.add))
            return done["acc"]

        def pipeline(stages):
            for n in range(TILES + len(stages) - 1):
                for k, stage in reversed(list(enumerate(stages))):
                    if 0 <= n - k < TILES:
                        stage(n - k)

        marks = {}

        wait(P, k_w)

        def l0_norm(t):
            marks["h", t] = norm(t, [k_x, k_const], hbuf[:, t % 2, :], marks.get(("hread", t - 2)))

        def l0_tr(t):
            marks["hread", t], marks["hT", t] = transposed(t, hbuf[:, t % 2, :], marks["h", t])

        def l0_mm(t):
            m = project(t, marks["hT", t], wbuf)
            free["hT", t % 2] = m
            wait(V, m, marks.get(("st", t - 3)))
            free["bankZ", t % 2] = m = c_v.after(V.tensor_copy(zbuf[:, t % 3, :], bank[6 + t % 2][0:TN, :]))
            marks["st", t] = store(t, table[0], zbuf[:, t % 3, :], m)

        wait(V, k_dis)
        pipeline([l0_norm, l0_tr, l0_mm])
        stored = [marks["st", t] for t in range(TILES - 3, TILES)]
        m = c_v.after(V.memset(acc[:, :, :], 0.0))
        wait(G, k_tables)
        k_acc = aggregate(0, acc, True, stored, [m])

        w_raw = ring[:, 0:KB, :]
        wait(S, done["pe"][-1])
        m = c_w.after(S.dma_start(w_raw, W1_in.rearrange("(k p) d -> p k d", p=128)), 16)
        k_b = c_w.after(S.dma_start(bias_bc[:, :], b1_in.rearrange("(a d) -> a d", a=1).to_broadcast([TN, D])), 16)
        wait(P, k_b)
        for k in range(KB):
            wait(P, free.get(("bankT", k % 2)))
            for j in range(KB):
                last = P.transpose(bank[4 + k % 2][:, j * 128:(j + 1) * 128], w_raw[:, j, k * 128:(k + 1) * 128], ident[:, :])
            m = c_p.after(last)
            wait(V, m)
            k_w = free["bankT", k % 2] = c_v.after(V.tensor_copy(wbuf[:, k, :], bank[4 + k % 2][:, :]))
        wait(P, k_w)
        wait(V, k_b, k_acc)

        def l1_norm(t):
            m = c_v.after(V.scalar_tensor_tensor(out=x[:, t, :], in0=acc[:, t, :], scalar=0.0, in1=x[:, t, :],
                                                 op0=ALU.max, op1=ALU.add))
            marks["h", t] = norm(t, [m], hbuf[:, t % 2, :], marks["hread", (t - 2) % TILES])

        def l1_mm(t):
            m = project(t, marks["hT", t], wbuf)
            free["hT", t % 2] = m
            wait(V, m, marks.get(("scaled", t - 3)))
            free["bankZ", t % 2] = m = c_v.after(V.tensor_tensor(zbuf[:, t % 3, :], bank[6 + t % 2][0:TN, :], bias_bc[:, :], ALU.add))
            wait(A, m)
            marks["scaled", t] = m = c_a.after(A.activation(acc[:, t, :], zbuf[:, t % 3, :], ACT.Copy, scale=dis[:, t:t + 1]))
            marks["st", t] = store(t, table[1], acc[:, t, :], m)

        wait(V, *stored)
        pipeline([l1_norm, l0_tr, l1_mm])
        stored = [marks["st", t] for t in range(TILES - 3, TILES)]
        k_acc = aggregate(1, acc, False, stored, stored)

        wait(A, k_acc)
        wait(V, k_acc)

        def l2_relu(t):
            wait(A, marks.get(("xadd", t - 2)))
            m = c_a.after(A.activation(hbuf[:, t % 2, :], acc[:, t, :], ACT.Relu, scale=dis[:, t:t + 1]))
            wait(V, m)
            marks["xadd", t] = c_v.after(V.tensor_tensor(x[:, t, :], x[:, t, :], hbuf[:, t % 2, :], ALU.add))

        def l2_norm(t):
            m = norm(t, [marks["xadd", t]], acc[:, t, :])
            marks["st", t] = store(t, table[2], acc[:, t, :], m)

        pipeline([l2_relu, l2_norm])
        stored = [marks["st", t] for t in range(TILES - 3, TILES)]
        k_acc = aggregate(2, acc, False, stored, stored)

        G2 = ring[:, KB:2 * KB, :]
        wait(S, done["pe"][-1])
        c_w.after(S.dma_start(wbuf[:, :, :], G1_in.rearrange("(k p) d -> p k d", p=128)), 16)
        c_w.after(S.dma_start(G2, G2_in.rearrange("(k p) d -> p k d", p=128)), 16)
        c_w.after(S.dma_start(bias_bc[:, :], g2_in.rearrange("(a d) -> a d", a=1).to_broadcast([TN, D])), 16)
        g1row = sb("g1row", [KB, 128])
        k_w = c_w.after(S.dma_start(g1row[:, :], g1_in.rearrange("(k p) -> k p", p=128)), 16)
        wait(P, k_w, k_acc)
        m = c_p.after(P.transpose(bank[0][:, 0:KB], g1row[:, :], ident[0:KB, 0:KB]))
        wait(V, m, k_w, k_acc)
        m = c_v.after(V.tensor_copy(g1col[:, :], bank[0][:, 0:KB]))
        wait(A, m)
        z1T = ring[:, 2 * KB:2 * KB + 2, 0:KB * TN].rearrange("p q (k n) -> p q k n", k=KB)

        def g_tr(t):
            _, marks["hT", t] = transposed(t, acc[:, t, :], None)

        def g_mm1(t):
            q = t % 2
            wait(P, marks["hT", t], marks.get(("z1", t - 2)))
            for j in range(KB):
                for k in range(KB):
                    last = P.matmul(bank[q][:, j * TN:(j + 1) * TN], wbuf[:, k, j * 128:(j + 1) * 128], hT[:, q, k, :],
                                    start=(k == 0), stop=(k == KB - 1))
            m = free["hT", q] = c_p.after(last)
            wait(A, m, marks.get(("mm2", t - 2)))
            for j in range(KB):
                last = A.activation(z1T[:, q, j, :], bank[q][:, j * TN:(j + 1) * TN], ACT.Relu, bias=g1col[:, j:j + 1])
            marks["z1", t] = c_a.after(last)

        def g_mm2(t):
            q = t % 2
            wait(P, marks["z1", t], free.get(("bankZ", q)))
            for k in range(KB):
                last = P.matmul(bank[6 + q][0:TN, :], z1T[:, q, k, :], G2[:, k, :], start=(k == 0), stop=(k == KB - 1))
            m = marks["mm2", t] = c_p.after(last)
            m2 = c_v.after(V.tensor_tensor(x[:, t, :], x[:, t, :], bias_bc[:, :], ALU.add))
            wait(V, m, m2)
            free["bankZ", q] = marks["x", t] = c_v.after(V.tensor_tensor(x[:, t, :], x[:, t, :], bank[6 + q][0:TN, :], ALU.add))

        pipeline([g_tr, g_mm1, g_mm2])
        k_x3 = marks["x", TILES - 1]

        wait(S, k_x3)
        c_w.after(S.dma_start(wbuf[:, :, :].rearrange("p k (h j) -> p k h j", h=H)[:, 0, :, :],
                              Ws_in[:, 0:128, :].rearrange("h p j -> p h j")), 16)
        for k in range(1, KB):
            c_w.after(S.dma_start(wbuf[:, k, :].rearrange("p (h j) -> p h j", h=H),
                                  Ws_in[:, k * 128:(k + 1) * 128, :].rearrange("h p j -> p h j")), 16)
        aw_bc = ring[:, 0:2, :].rearrange("p s (h j) -> p s h j", h=H)
        for s in range(2):
            c_w.after(S.dma_start(aw_bc[:, s, :, :], aw_in[:, s * DP:(s + 1) * DP].rearrange("(a h) j -> a h j", a=1)
                                  .to_broadcast([128, H, DP])), 16)
        c_w.after(S.dma_start(bias_bc[:, :], Wb_in.rearrange("(a h) j -> a (h j)", a=1).to_broadcast([TN, D])), 16)
        ab_bc = sb("ab_bc", [TN, H])
        k_w = c_w.after(S.dma_start(ab_bc[:, :], ab_in.rearrange("(a h) -> a h", a=1).to_broadcast([TN, H])), 16)
        wait(P, k_w)
        wait(V, k_w)
        prod = ring[:, 2, :].rearrange("p (h j) -> p h j", h=H)
        for s in range(2):
            for k in range(KB):
                m = c_v.after(V.tensor_tensor(prod, wbuf[:, k, :].rearrange("p (h j) -> p h j", h=H), aw_bc[:, s, :, :], ALU.mult))
                wait(V, m)
                m = c_v.after(V.tensor_reduce(wa[:, k, s * H:(s + 1) * H], prod, axis=AX.X, op=ALU.add))
                wait(V, m)
            m = c_v.after(V.tensor_tensor(prod[0:TN], bias_bc[:, :].rearrange("p (h j) -> p h j", h=H), aw_bc[0:TN, s, :, :], ALU.mult))
            wait(V, m)
            m = c_v.after(V.tensor_reduce(sc_bias[:, s * H:(s + 1) * H], prod[0:TN], axis=AX.X, op=ALU.add))
            wait(V, m)
        k_wa = c_v.after(V.tensor_tensor(sc_bias[:, 0:H], sc_bias[:, 0:H], ab_bc[:, :], ALU.add))
        wait(P, k_wa)
        wait(V, k_wa)
        c_us = [count(f"c_us{n}") for n in range(2)]

        def l3_norm(t):
            marks["h", t] = norm(t, [], hbuf[:, t % 2, :], marks.get(("hread3", t - 2)))

        def l3_tr(t):
            marks["hread3", t], marks["hT", t] = transposed(t, hbuf[:, t % 2, :], marks["h", t])

        def l3_mm(t):
            q = t % 2
            m = project(t, marks["hT", t], wbuf)
            wait(P, marks.get(("sc", t - 2)))
            for k in range(KB):
                last = P.matmul(bank[q][0:TN, 0:2 * H], hT[:, q, k, :], wa[:, k, :], start=(k == 0), stop=(k == KB - 1))
            m = free["hT", q] = c_p.after(last)
            wait(V, m, marks.get(("st3", t - 3)), marks.get(("us", t - 2)))
            m = free["bankZ", q] = c_v.after(V.tensor_tensor(zbuf[:, t % 3, :], bank[6 + q][0:TN, :], bias_bc[:, :], ALU.add))
            m2 = c_v.after(V.tensor_tensor(scb[:, q, :], bank[q][0:TN, 0:2 * H], sc_bias[:, :], ALU.add))
            marks["sc", t] = m2
            wait(V, m2)
            marks["t_all"] = c_v.after(V.tensor_copy(t_all[:, t, :], scb[:, q, 0:H]))
            marks["st3", t] = store(t, table[3], zbuf[:, t % 3, :], m)
            wait(S, m2)
            marks["us", t] = c_us[q].after(S.dma_start(score_table[t * TN:(t + 1) * TN, :], scb[:, q, H:2 * H]), 16)

        pipeline([l3_norm, l3_tr, l3_mm])
        stored = [marks["st3", t] for t in range(TILES - 3, TILES)]
        stored_u = [marks["us", t] for t in range(TILES - 2, TILES)]

        pool = acc[:, :, :].rearrange("p a b -> p (a b)")
        WR = RB * H * CE
        ue = sb("ue", [CE, STEPS, H])
        te = ring[:, :, :].rearrange("p a b -> p (a b)")[:, 4096:4096 + STEPS * H].rearrange("p (i h) -> p i h", h=H)
        wait(G, *stored_u, k_x3)
        for i in range(STEPS):
            k_ue = c_gl.after(G.indirect_dma_start(out=ue[:, i, :], out_offset=None, in_=score_table[:, :],
                                                   in_offset=bass.IndirectOffsetOnAxis(ap=src_t[:, i:i + 1], axis=0)), 16)
        selT = zbuf[:, 0, :].rearrange("p (a b) -> p a b", b=CE)
        wait(A, *stored)
        wait(P, marks["t_all"], marks["sc", TILES - 1], marks["sc", TILES - 2])
        tb = {}
        PB = 512 // H
        for i in range(STEPS):
            q = i % 4
            if i >= 4:
                wait(V, tb["tr", i - 4])
            m = c_v.after(V.tensor_scalar(out=sel[:, q, :], in0=node_iota[:, :], scalar1=dl_t[:, i:i + 1],
                                          scalar2=None, op0=ALU.is_equal))
            wait(P, m, tb.get(("cp", i - 2)), free.get(("bankT", 0)), free.get(("bankT", 1)))
            m = tb["tr", i] = c_p.after(P.transpose(bank[4 + i % 2][0:TN, 0:CE], sel[:, q, :], ident[:, :]))
            wait(A, m, tb.get(("te", i - 4)))
            m = tb["cp", i] = c_a.after(A.copy(selT[:, q, :], bank[4 + i % 2][0:TN, 0:CE]))
            t = P.value_load(tile_row[0:1, i:i + 1], min_val=0, max_val=TILES - 1)
            gb, gi = divmod(i, PB)
            if gi == 0:
                wait(P, tb.get(("bk", gb - 2)))
            wait(P, m)
            m = tb["te", i] = c_p.after(P.matmul(bank[gb % 2][:, gi * H:(gi + 1) * H], selT[:, q, :],
                                                 t_all[:, bass.ds(t, 1), :].rearrange("p a h -> p (a h)"), start=True, stop=True))
            if gi == PB - 1 or i == STEPS - 1:
                wait(V, m)
                k_te = tb["bk", gb] = c_v.after(V.tensor_copy(te[:, gb * PB:i + 1, :].rearrange("p a h -> p (a h)"),
                                                              bank[gb % 2][:, 0:(gi + 1) * H]))

        ur = pool[0:RS, 0:WR].rearrange("p (b h e) -> p b h e", b=RB, h=H)
        tr = pool[0:RS, WR:2 * WR].rearrange("p (b h e) -> p b h e", b=RB, h=H)
        fr = pool[0:RS, 2 * WR:3 * WR].rearrange("p (b h e) -> p b h e", b=RB, h=H)
        rg = ring[0:RS, :, :].rearrange("p a b -> p (a b)")
        keep = rg[:, 0:RB * CE].rearrange("p (b e) -> p b e", b=RB)
        nlast = rg[:, RB * CE:2 * RB * CE].rearrange("p (b e) -> p b e", b=RB)
        pf = rg[:, 2 * RB * CE:3 * RB * CE].rearrange("p (b e) -> p b e", b=RB)
        pb_ = rg[:, 3 * RB * CE:4 * RB * CE].rearrange("p (b e) -> p b e", b=RB)
        kbig = rg[:, 4 * RB * CE:5 * RB * CE].rearrange("p (b e) -> p b e", b=RB)
        pfb = rg[:, 5 * RB * CE:6 * RB * CE].rearrange("p (b e) -> p b e", b=RB)
        lastf = rg[:, 6 * RB * CE:7 * RB * CE].rearrange("p (b e) -> p b e", b=RB)
        zero = sb("zero", [RS, CE])
        edge8 = sb("edge8", [RS, RB, 4, H])
        row8 = sb("row8", [H, 4, STEPS + 2])
        r8x = sb("r8x", [H, STEPS])
        back8 = sb("back8", [RS, RB, 2, H])
        tq = {"n": 0}
        bank_free = {}

        def through(in_ap, out_ap, np_in, nf_in, ready):
            b = 4 + tq["n"] % 4
            tq["n"] += 1
            wait(P, ready, bank_free.get(b))
            m = c_p.after(P.transpose(bank[b][0:nf_in, 0:np_in], in_ap, ident[0:np_in, 0:np_in]))
            if tq["n"] % 2:
                wait(V, m)
                bank_free[b] = c_v.after(V.tensor_copy(out_ap, bank[b][0:nf_in, 0:np_in]))
            else:
                wait(A, m)
                bank_free[b] = c_a.after(A.copy(out_ap, bank[b][0:nf_in, 0:np_in]))
            return bank_free[b]

        def join():
            for e in (V, A, P, G):
                for c in (c_v, c_a, c_p):
                    wait(e, (c.sem, c.value))

        join()
        wait(P, k_ue)
        c_v.after(V.tensor_tensor(keep[:, :, 1:CE], dstf[:, :, 1:CE], dstf[:, :, 0:CE - 1], ALU.is_equal))
        c_v.after(V.tensor_copy(edge8[:, :, 0, :], dstf[:, :, 0:1].to_broadcast([RS, RB, H])))
        c_v.after(V.tensor_copy(edge8[:, :, 1, :], dstf[:, :, CE - 1:CE].to_broadcast([RS, RB, H])))
        c_v.after(V.memset(row8[:, :, :], -1.0))
        c_v.after(V.memset(zero[:, :], 0.0))
        join()
        for b in range(RB):
            for s in range(2):
                through(edge8[:, b, s, :], row8[:, s, 1 + s + b * RS:1 + s + (b + 1) * RS], RS, H, None)
        join()
        c_v.after(V.memset(row8[:, 2, :], 0.0))
        join()
        c_v.after(V.tensor_tensor(row8[:, 2, 1:STEPS + 1], row8[:, 0, 1:STEPS + 1], row8[:, 1, 1:STEPS + 1], ALU.is_equal))
        join()
        for b in range(RB):
            through(row8[:, 2, 1 + b * RS:1 + (b + 1) * RS], back8[:, b, 0, :], H, RS, None)
            through(row8[:, 2, 2 + b * RS:2 + (b + 1) * RS], back8[:, b, 1, :], H, RS, None)
        join()
        c_v.after(V.tensor_copy(keep[:, :, 0:1], back8[:, :, 0, 0:1]))
        c_v.after(V.tensor_copy(nlast[:, :, CE - 1:CE], back8[:, :, 1, 0:1]))
        c_v.after(V.tensor_copy(nlast[:, :, 0:CE - 1], keep[:, :, 1:CE]))
        join()
        for b in range(RB):
            c_v.after(V.tensor_tensor_scan(pf[:, b, :], keep[:, b, :], zero[:, :], 1.0, ALU.mult, ALU.add))
            c_v.after(V.tensor_tensor_scan(pb_[:, b, ::-1], nlast[:, b, ::-1], zero[:, :], 1.0, ALU.mult, ALU.add))
        c_v.after(V.tensor_scalar(out=lastf, in0=nlast, scalar1=-1.0, scalar2=1.0, op0=ALU.mult, op1=ALU.add))
        c_v.after(V.tensor_scalar(out=kbig, in0=keep, scalar1=-1.0, scalar2=BIG, op0=ALU.add, op1=ALU.mult))
        join()
        c_v.after(V.tensor_scalar(out=pfb, in0=pf, scalar1=-1.0, scalar2=BIG, op0=ALU.add, op1=ALU.mult))
        c_v.after(V.tensor_copy(edge8[:, :, 0, :], pf[:, :, CE - 1:CE].to_broadcast([RS, RB, H])))
        c_v.after(V.tensor_copy(edge8[:, :, 1, :], pb_[:, :, 0:1].to_broadcast([RS, RB, H])))
        join()
        for b in range(RB):
            for s in range(2):
                through(edge8[:, b, s, :], row8[:, 2 + s, 1 + b * RS:1 + (b + 1) * RS], RS, H, None)
        for b in range(RB):
            for h in range(H):
                through(ue[:, b * RS:(b + 1) * RS, h], ur[:, b, h, :], CE, RS, None)
                through(te[:, b * RS:(b + 1) * RS, h], tr[:, b, h, :], CE, RS, None)
        join()

        def carry_to_rows(lane):
            for b in range(RB):
                through(r8x[:, b * RS:(b + 1) * RS], back8[:, b, lane, :], H, RS, None)

        def segment_total(data, sums):
            for b in range(RB):
                for h in range(H):
                    if sums:
                        c_v.after(V.tensor_tensor_scan(fr[:, b, h, :], keep[:, b, :], data[:, b, h, :], 0.0, ALU.mult, ALU.add))
                    else:
                        c_v.after(V.tensor_tensor_scan(fr[:, b, h, :], kbig[:, b, :], data[:, b, h, :], -BIG, ALU.add, ALU.max))
            join()
            for b in range(RB):
                c_v.after(V.tensor_copy(edge8[:, b, 0, :], fr[:, b, :, CE - 1]))
            join()
            for b in range(RB):
                through(edge8[:, b, 0, :], row8[:, 0, 1 + b * RS:1 + (b + 1) * RS], RS, H, None)
            join()
            if sums:
                c_v.after(V.memset(r8x[:, 0:1], 0.0))
                c_v.after(V.tensor_tensor_scan(r8x[:, 1:STEPS], row8[:, 2, 1:STEPS], row8[:, 0, 1:STEPS], 0.0, ALU.mult, ALU.add))
            else:
                c_v.after(V.tensor_scalar(out=row8[:, 1, :], in0=row8[:, 2, :], scalar1=-1.0, scalar2=BIG, op0=ALU.add, op1=ALU.mult))
                c_v.after(V.memset(r8x[:, 0:1], -BIG))
                join()
                c_v.after(V.tensor_tensor_scan(r8x[:, 1:STEPS], row8[:, 1, 1:STEPS], row8[:, 0, 1:STEPS], -BIG, ALU.add, ALU.max))
            join()
            carry_to_rows(0)
            join()
            for b in range(RB):
                for h in range(H):
                    if sums:
                        c_v.after(V.scalar_tensor_tensor(out=fr[:, b, h, :], in0=pf[:, b, :], scalar=back8[:, b, 0, h:h + 1],
                                                         in1=fr[:, b, h, :], op0=ALU.mult, op1=ALU.add))
                    else:
                        c_v.after(V.scalar_tensor_tensor(out=fr[:, b, h, :], in0=pfb[:, b, :], scalar=back8[:, b, 0, h:h + 1],
                                                         in1=fr[:, b, h, :], op0=ALU.add, op1=ALU.max))
            join()
            c_v.after(V.tensor_tensor(fr, fr, lastf[:, :, None, :].to_broadcast([RS, RB, H, CE]), ALU.mult))
            join()
            for b in range(RB):
                for h in range(H):
                    c_v.after(V.tensor_tensor_scan(data[:, b, h, ::-1], nlast[:, b, ::-1], fr[:, b, h, ::-1], 0.0, ALU.mult, ALU.add))
            join()
            for b in range(RB):
                c_v.after(V.tensor_copy(edge8[:, b, 0, :], data[:, b, :, 0]))
            join()
            for b in range(RB):
                through(edge8[:, b, 0, :], row8[:, 0, 1 + b * RS:1 + (b + 1) * RS], RS, H, None)
            join()
            c_v.after(V.memset(r8x[:, STEPS - 1:STEPS], 0.0))
            c_v.after(V.tensor_tensor_scan(r8x[:, 0:STEPS - 1][:, ::-1], row8[:, 3, 2:STEPS + 1][:, ::-1],
                                           row8[:, 0, 2:STEPS + 1][:, ::-1], 0.0, ALU.mult, ALU.add))
            join()
            carry_to_rows(1)
            join()
            for b in range(RB):
                for h in range(H):
                    c_v.after(V.scalar_tensor_tensor(out=data[:, b, h, :], in0=pb_[:, b, :], scalar=back8[:, b, 1, h:h + 1],
                                                     in1=data[:, b, h, :], op0=ALU.mult, op1=ALU.add))
            join()

        fl = lambda v: v.rearrange("p b h e -> p (b h e)")
        ex = rg[:, 4096:8192].rearrange("p (b h e) -> p b h e", b=RB, h=H)
        c_v.after(V.tensor_tensor(fl(ex[:, :, :, :]), fl(ur), fl(tr), ALU.add))
        join()
        c_v.after(V.scalar_tensor_tensor(out=fl(ex[:, :, :, :]), in0=fl(ex[:, :, :, :]), scalar=0.2, in1=fl(ex[:, :, :, :]),
                                         op0=ALU.mult, op1=ALU.max))
        segment_total(ur, False)
        c_v.after(V.tensor_tensor(fl(ur), fl(ur), fl(tr), ALU.add))
        join()
        c_v.after(V.scalar_tensor_tensor(out=fl(ur), in0=fl(ur), scalar=0.2, in1=fl(ur), op0=ALU.mult, op1=ALU.max))
        join()
        c_v.after(V.tensor_tensor(fl(ex[:, :, :, :]), fl(ex[:, :, :, :]), fl(ur), ALU.subtract))
        join()
        c_a.after(A.activation(fl(ex[:, :, :, :]), fl(ex[:, :, :, :]), ACT.Exp))
        join()
        c_v.after(V.tensor_tensor(ex[:, :, :, :], ex[:, :, :, :], valid[:, :, None, :].to_broadcast([RS, RB, H, CE]), ALU.mult))
        join()
        c_v.after(V.tensor_copy(fl(ur), fl(ex[:, :, :, :])))
        join()
        segment_total(ur, True)
        c_v.after(V.tensor_scalar(out=fl(ur), in0=fl(ur), scalar1=0.5, scalar2=None, op0=ALU.max))
        join()
        c_v.after(V.reciprocal(fl(ur), fl(ur)))
        join()
        c_v.after(V.tensor_tensor(fl(ur), fl(ur), fl(ex[:, :, :, :]), ALU.mult))
        join()
        alpha = ue
        for b in range(RB):
            for h in range(H):
                through(ur[:, b, h, :], alpha[:, b * RS:(b + 1) * RS, h], RS, CE, None)
        join()
        aggregate(3, x, False, stored, [], alpha=alpha)
        wait(S, done["acc"])
        k_out = c_out.after(S.dma_start(out.rearrange("(t p) d -> p t d", p=TN), x[:, :, :]), 16)
        wait(S, k_out)


INPUTS = ["x", "src", "dst", "edge_weight", "L0_gnn_W", "L1_gnn_W", "L1_gnn_b", "L2_gnn_W1", "L2_gnn_b1",
          "L2_gnn_W2", "L2_gnn_b2", "L3_gnn_Ws", "L3_gnn_Wb", "L3_gnn_a_w", "L3_gnn_a_b"]


def kernel(**inputs):
    import concourse.bacc as bacc
    from concourse.bass_utils import run_bass_kernel_spmd as run

    nc = bacc.Bacc("TRN2", target_bir_lowering=False, num_devices=1)
    arrays, args = {}, []
    for name in INPUTS:
        a = np.ascontiguousarray(inputs[name])
        arrays["in_" + name] = a
        args.append(nc.dram_tensor("in_" + name, a.shape, mybir.dt.from_np(a.dtype), kind="ExternalInput").ap())
    result = nc.dram_tensor("out_0", inputs["x"].shape, F32, kind="ExternalOutput").ap()
    build(nc, *args, result)
    r = run(nc, [arrays], core_ids=[0])
    return r.results[0]["out_0"]
```

```python
import numpy as np
import concourse.bass as bass
from concourse import mybir
from contextlib import ExitStack

F32 = mybir.dt.float32
I32 = mybir.dt.int32
F32R = mybir.dt.float32r
BF16 = mybir.dt.bfloat16
ALU = mybir.AluOpType
ACT = mybir.ActivationFunctionType
AX = mybir.AxisListType


class Count:

    def __init__(self, sem):
        self.sem, self.value = sem, 0

    def after(self, instruction, by=1):
        instruction.then_inc(self.sem, by)
        self.value += by
        return (self.sem, self.value)


def build(nc, x_in, src_in, dst_in, w_in, W0_in, W1_in, b1_in, G1_in, g1_in, G2_in, g2_in,
          Ws_in, Wb_in, aw_in, ab_in, out):
    N, D = x_in.shape
    E = src_in.shape[0]
    H, _, DP = Ws_in.shape
    TN = 125
    TILES = N // TN
    CE = 128
    CHUNKS = -(-E // CE)
    STEPS = CHUNKS + TILES - 1
    RB = 4
    RS = STEPS // RB
    KB = D // 128
    EC = 4
    EP = CHUNKS // EC
    EROW = EC * CE
    RING = 12
    SELS = 8
    AHEAD = 4
    SCALE_AHEAD = 2
    NAGG = 4
    EPS = 1e-5
    BIG = 1e30
    FAR = 1 << 20
    SLOPE = 0.2
    assert TILES * TN == N and RB * RS == STEPS and EP * EC == CHUNKS and KB * 128 == D and H * DP == D

    ctx = ExitStack()
    with ctx:
        def sb(name, shape, dt=F32):
            return ctx.enter_context(nc.sbuf_tensor(name, shape, dt))

        def count(name):
            return Count(ctx.enter_context(nc.semaphore(name)))

        V, A, P, G, S = nc.vector, nc.scalar, nc.tensor, nc.gpsimd, nc.sync

        def wait(engine, *marks):
            for mark in marks:
                if mark is not None:
                    engine.wait_ge(*mark)

        edge_rows = nc.dram_tensor("edge_rows", (CHUNKS, 3 * CE), I32, kind="Internal").ap()
        table = [nc.dram_tensor(f"table{n}", (N, D), F32, kind="Internal").ap() for n in range(4)]
        score_table = nc.dram_tensor("score_table", (N, H), F32, kind="Internal").ap()

        x = sb("x", [128, TILES, D])
        acc = sb("acc", [128, TILES, D])
        ring = sb("ring", [CE, RING, D])
        big = sb("big", [128, 5632])
        stage = sb("stage", [128, 5 * D])
        sel = sb("sel", [CE, SELS, TN])
        wh = sb("wh", [128, KB, D], F32R)
        wl = sb("wl", [128, KB, D], F32R)
        hTh = sb("hTh", [128, 2, KB, TN], F32R)
        hTl = sb("hTl", [128, 2, KB, TN], F32R)
        ident = sb("ident", [128, 128])
        node_iota = sb("node_iota", [128, TN])
        ones = sb("ones", [128, 128])
        eps = sb("eps", [128, 1])
        src_t = sb("src_t", [CE, STEPS], I32)
        dl_t = sb("dl_t", [CE, STEPS])
        w_t = sb("w_t", [CE, STEPS])
        tile_row = sb("tile_row", [1, STEPS], I32)
        dstf = sb("dstf", [RS, RB, CE])
        masked = sb("masked", [RS, RB, CE])
        dis = sb("dis", [TN, TILES])
        stats = sb("stats", [TN, 4, 6])
        mv = sb("mv", [TN, 4, 2])
        rstd = sb("rstd", [TN, 4, 2])
        bias_bc = sb("bias_bc", [TN, D])
        wa = sb("wa", [128, KB, 2 * H])
        u_out = sb("u_out", [TN, 2, H])
        sc_bias = sb("sc_bias", [TN, 2 * H])
        ab_bc = sb("ab_bc", [TN, H])
        t_all = sb("t_all", [TN, TILES, H])
        edge8 = sb("edge8", [RS, RB, 2, H])
        back8 = sb("back8", [RS, RB, 2, H])

        flat_ring = ring[:, :, :].rearrange("p a b -> p (a b)")

        def hbuf(q):
            return stage[0:TN, q * D:(q + 1) * D]

        def zbuf(q):
            return stage[0:TN, (2 + q) * D:(3 + q) * D]

        raw_w = stage[:, 0:KB * D].rearrange("p (k d) -> p k d", k=KB)

        bank = [ctx.enter_context(nc.psum_tensor(f"bank{n}", [128, 512], F32)) for n in range(8)]

        c_v, c_a, c_p, c_g = count("c_v"), count("c_a"), count("c_p"), count("c_g")
        c_ld = count("c_ld")
        c_lx = count("c_lx")
        c_er = count("c_er")
        c_pt = count("c_pt")
        c_w = count("c_w")
        c_w2 = count("c_w2")
        c_st = [count(f"c_st{n}") for n in range(3)]
        c_us = [count(f"c_us{n}") for n in range(2)]
        c_ring = [count(f"c_ring{n}") for n in range(RING)]
        c_ue = [count(f"c_ue{n}") for n in range(RB)]
        c_out = [count(f"c_out{n}") for n in range(5)]

        m = c_g.after(G.memset(ident[:, :], 0.0))
        wait(G, m)
        k_ident = c_g.after(G.affine_select(out=ident[:, :], in_=ident[:, :], compare_op=ALU.not_equal,
                                            fill=1.0, base=0, pattern=[[-1, 128]], channel_multiplier=1))
        iota_i = sb("iota_i", [128, TN], I32)
        m = c_g.after(G.iota(iota_i[:, :], pattern=[[1, TN]], base=0, channel_multiplier=0))
        step_i = sb("step_i", [RS, RB], I32)
        step_f = sb("step_f", [RS, RB])
        c_g.after(G.iota(step_i[:, :], pattern=[[RS, RB]], base=0, channel_multiplier=1))
        tile_i = sb("tile_i", [128, TILES - 1], I32)
        tile_f = sb("tile_f", [128, TILES - 1])
        k_iota = c_g.after(G.iota(tile_i[:, :], pattern=[[CE, TILES - 1]], base=CE, channel_multiplier=0))

        ed = flat_ring[0:EP, 0:3 * D].bitcast(I32).rearrange("p (c a e) -> p c a e", c=EC, a=3)
        edf = flat_ring[0:EP, 0:3 * D].rearrange("p (c a e) -> p c a e", c=EC, a=3)
        k_x = []
        XQ = TILES // 5

        def load_x(engine, q):
            k_x.append(count(f"c_lx{q}").after(engine.dma_start(
                x[0:TN, q * XQ:(q + 1) * XQ, :],
                x_in[q * XQ * TN:(q + 1) * XQ * TN, :].rearrange("(t p) d -> p t d", p=TN)), 16))

        load_x(A, 0)
        k_w = c_w.after(A.dma_start(flat_ring[:, 7 * D:11 * D].rearrange("p (k d) -> p k d", k=KB),
                                    W0_in.rearrange("(k p) d -> p k d", p=128)), 16)
        for a, value in ((0, 0), (1, FAR), (2, 0)):
            k_pad = c_v.after(V.memset(ed[:, :, a, :], value))
        wait(S, k_pad)
        full = E // EROW
        rest = E - full * EROW
        rc = rest // CE
        for a, arr in enumerate((src_in, dst_in, w_in)):
            e = edf if a == 2 else ed
            k_ed = c_ld.after(S.dma_start(e[0:full, :, a, :], arr[0:full * EROW].rearrange(
                "(p c e) -> p c e", c=EC, e=CE)), 16)
            if rc:
                k_ed = c_ld.after(S.dma_start(e[full:full + 1, 0:rc, a, :], arr[full * EROW:full * EROW + rc * CE]
                                              .rearrange("(p c e) -> p c e", p=1, e=CE)), 16)
            if rest % CE:
                k_ed = c_ld.after(S.dma_start(e[full:full + 1, rc, a, 0:rest % CE],
                                              arr[full * EROW + rc * CE:E].rearrange("(p e) -> p e", p=1)), 16)
        for q in range(1, 5):
            load_x(S, q)
        wait(S, k_ed)
        k_er = c_er.after(S.dma_start(edge_rows.rearrange("(p c) e -> p (c e)", c=EC),
                                      ed.rearrange("p c a e -> p (c a e)")), 16)
        wait(V, k_iota)
        c_v.after(V.tensor_copy(node_iota[:, :], iota_i[:, :]))
        c_v.after(V.tensor_copy(step_f[:, :], step_i[:, :]))
        c_v.after(V.tensor_copy(tile_f[:, :], tile_i[:, :]))
        c_v.after(V.memset(ones[:, :], 1.0))
        k_const = c_v.after(V.memset(eps[:, :], EPS))
        wait(V, k_const)

        def step_tables():
            df = flat_ring[0:EP, 3 * D:4 * D]
            junk = flat_ring[0:EP, 4 * D:5 * D]
            cnt = sb("cnt", [EP, TILES - 1])
            wait(V, k_ed)
            m = c_v.after(V.tensor_copy(df.rearrange("p (c e) -> p c e", c=EC), ed[:, :, 1, :]))
            wait(V, m)
            for t in range(1, TILES):
                m = c_v.after(V.tensor_scalar(out=junk, in0=df, scalar1=float(t * TN), scalar2=None, op0=ALU.is_lt,
                                              op1=ALU.add, accum_out=cnt[:, t - 1:t]))
                wait(V, m)
                if t % 2 == 0:
                    yield
            wait(P, m)
            m = c_p.after(P.matmul(bank[0][:, 0:TILES - 1], ones[0:EP, :], cnt[:, :], start=True, stop=True))
            thr = sb("thr", [128, TILES - 1])
            lim = sb("lim", [RS, RB])
            tstep = sb("tstep", [RS, RB])
            tn_step = sb("tn_step", [RS, RB])
            gstep = sb("gstep", [RS, RB], I32)
            thr_junk = sb("thr_junk", [RS, TILES - 1])
            wait(V, m)
            c_v.after(V.tensor_tensor(thr[:, :], bank[0][:, 0:TILES - 1], tile_f[:, :], ALU.add))
            m = c_v.after(V.tensor_scalar(out=lim[:, :], in0=step_f[:, :], scalar1=1.0, scalar2=float(CE),
                                          op0=ALU.add, op1=ALU.mult))
            wait(V, m)
            for b in range(RB):
                m = c_v.after(V.tensor_scalar(out=thr_junk[:, :], in0=thr[0:RS, :], scalar1=lim[:, b:b + 1], scalar2=None,
                                              op0=ALU.is_lt, op1=ALU.add, accum_out=tstep[:, b:b + 1]))
                wait(V, m)
            c_v.after(V.tensor_scalar(out=tn_step[:, :], in0=tstep[:, :], scalar1=float(TN), scalar2=None, op0=ALU.mult))
            k_g = c_v.after(V.tensor_tensor(gstep[:, :], step_f[:, :], tstep[:, :], ALU.subtract))
            rows = [flat_ring[0:RS, (3 + b) * D:(3 + b) * D + 3 * CE] for b in range(RB)]
            wait(G, k_g, k_er)
            for b in range(RB):
                k_pt = c_pt.after(G.indirect_dma_start(
                    out=rows[b].bitcast(I32), out_offset=None, in_=edge_rows[:, :],
                    in_offset=bass.IndirectOffsetOnAxis(ap=gstep[:, b:b + 1], axis=0)), 16)
            yield
            yield
            wait(V, k_pt, k_g)
            rsf = big[0:RS, 0:RB * 2 * CE].rearrange("p (b a e) -> p b a e", b=RB, a=2)
            for b in range(RB):
                ri = rows[b].bitcast(I32)
                c_v.after(V.tensor_copy(rsf[:, b, 0, :], ri[:, 0:CE]))
                c_v.after(V.tensor_scalar(out=rsf[:, b, 1, :], in0=ri[:, CE:2 * CE], scalar1=tn_step[:, b:b + 1],
                                          scalar2=None, op0=ALU.subtract))
                m = c_v.after(V.tensor_copy(dstf[:, b, :], ri[:, CE:2 * CE]))
            wait(V, m)
            wait(P, m, k_ident, k_pt)
            tb = [0, 1, 2, 3]
            for b in range(RB):
                for a in range(3):
                    piece = rows[b][:, 2 * CE:3 * CE] if a == 2 else rsf[:, b, a, :]
                    m = c_p.after(P.transpose(bank[tb[a]][:, b * RS:(b + 1) * RS], piece, ident[0:RS, 0:RS]))
                m = c_p.after(P.transpose(bank[tb[3]][0:1, b * RS:(b + 1) * RS], tstep[:, b:b + 1], ident[0:RS, 0:RS]))
            yield
            wait(V, m)
            c_v.after(V.tensor_copy(src_t[:, :], bank[tb[0]][:, 0:STEPS]))
            c_v.after(V.tensor_copy(dl_t[:, :], bank[tb[1]][:, 0:STEPS]))
            c_v.after(V.tensor_copy(w_t[:, :], bank[tb[2]][:, 0:STEPS]))
            marks["tables"] = c_v.after(V.tensor_copy(tile_row[:, :], bank[tb[3]][0:1, 0:STEPS]))
            wait(V, marks["tables"])
            m = c_v.after(V.tensor_scalar(out=masked[:, :, :], in0=rsf[:, :, 1, :], scalar1=0.0, scalar2=None, op0=ALU.is_ge))
            wait(V, m)
            m = c_v.after(V.scalar_tensor_tensor(out=masked[:, :, :], in0=rsf[:, :, 1, :], scalar=float(TN),
                                                 in1=masked[:, :, :], op0=ALU.is_lt, op1=ALU.mult))
            wait(V, m)
            m = marks["masked"] = c_v.after(V.tensor_scalar(out=masked[:, :, :], in0=masked[:, :, :], scalar1=-1.0,
                                                            scalar2=BIG, op0=ALU.add, op1=ALU.mult))
            wait(V, m)

        def degrees():
            hot = big[:, 0:TILES * STEPS // 2].bitcast(BF16).rearrange("p (t i) -> p t i", t=TILES)
            hi, lo, srcm = (stage[:, n * STEPS:(n + 1) * STEPS] for n in range(3))
            lo_hot = stage[:, 3 * STEPS:3 * STEPS + 4 * 64].bitcast(BF16).rearrange("p (q n) -> p q n", q=4)
            lo_abs = stage[:, 3 * STEPS + 4 * 64:3 * STEPS + 8 * 64].bitcast(BF16).rearrange("p (q n) -> p q n", q=4)
            m = c_v.after(V.tensor_scalar(out=srcm, in0=dl_t[:, :], scalar1=0.0, scalar2=None, op0=ALU.is_ge))
            wait(V, m)
            m = c_v.after(V.scalar_tensor_tensor(out=srcm, in0=dl_t[:, :], scalar=float(TN), in1=srcm, op0=ALU.is_lt, op1=ALU.mult))
            wait(V, m)
            m = c_v.after(V.tensor_scalar(out=srcm, in0=srcm, scalar1=-1.0, scalar2=-float(N), op0=ALU.add, op1=ALU.mult))
            yield
            wait(V, m)
            m = c_v.after(V.tensor_tensor(srcm, srcm, src_t[:, :], ALU.add))
            yield
            wait(V, m)
            m = c_v.after(V.tensor_scalar(out=hi, in0=srcm, scalar1=float(TN), scalar2=None, op0=ALU.is_ge))
            for t in range(2, TILES + 1):
                yield
                wait(V, m)
                m = c_v.after(V.scalar_tensor_tensor(out=hi, in0=srcm, scalar=float(t * TN), in1=hi, op0=ALU.is_ge, op1=ALU.add))
            yield
            wait(V, m)
            m = k_lo = c_v.after(V.scalar_tensor_tensor(out=lo, in0=hi, scalar=float(TN), in1=srcm, op0=ALU.mult, op1=ALU.subtract))
            for t in range(TILES):
                yield
                m = c_v.after(V.tensor_scalar(out=hot[:, t, :], in0=hi, scalar1=float(t), scalar2=None, op0=ALU.is_equal))
            wait(A, m, k_lo)
            wait(P, m)
            used = {}
            for i in range(STEPS):
                q = i % 4
                m = c_a.after(A.activation(lo_abs[:, q, 0:TN], node_iota[:, :], ACT.Abs, bias=lo[:, i:i + 1]))
                wait(A, m, used.get(i - 4))
                m = c_a.after(A.activation(lo_hot[:, q, 0:TN], lo_abs[:, q, 0:TN], ACT.Relu, bias=ones[:, 0:1], scale=-1.0))
                wait(P, m)
                used[i] = c_p.after(P.matmul(bank[4][0:TN, 0:TILES], lo_hot[:, q, 0:TN], hot[:, :, i],
                                             start=(i == 0), stop=(i == STEPS - 1)))
                if i % 3:
                    yield
            wait(V, used[STEPS - 1])
            m = c_v.after(V.tensor_scalar(out=dis[:, :], in0=bank[4][0:TN, 0:TILES], scalar1=1.0, scalar2=None, op0=ALU.add))
            free["bankT", 0] = m
            wait(A, m)
            m = c_a.after(A.activation(dis[:, :], dis[:, :], ACT.Sqrt))
            wait(V, m)
            marks["dis"] = c_v.after(V.reciprocal(dis[:, :], dis[:, :]))
            wait(A, marks["dis"])

        free = {}
        marks = {}

        def split(high, low, value, ready):
            wait(A, ready)
            m = c_a.after(A.copy(high, value))
            wait(V, ready, m)
            m2 = c_v.after(V.tensor_tensor(low, value, high.bitcast(F32), ALU.subtract))
            return m2

        def split_weight(high, low, raw, ready):
            for k in range(KB):
                m = split(high[:, k, :], low[:, k, :], raw[:, k, :], ready)
            return m

        def norm_stats(t, *before):
            q = t % 4
            wait(V, *before)
            m = c_v.after(V.bn_stats(stats[:, q, :], x[0:TN, t, :]))
            wait(V, m, free.get(("mv", q)))
            m = c_v.after(V.bn_aggr(mv[:, q, :], stats[:, q, :]))
            wait(A, m)
            marks["std", t] = c_a.after(A.activation(rstd[:, q, 0:1], mv[:, q, 1:2], ACT.Sqrt, bias=eps[0:TN, :]))

        def norm_relu(t, dest, dest_free=None):
            q = t % 4
            wait(V, marks["std", t])
            m = c_v.after(V.reciprocal(rstd[:, q, 0:1], rstd[:, q, 0:1]))
            wait(V, m)
            m = c_v.after(V.tensor_scalar(out=rstd[:, q, 1:2], in0=mv[:, q, 0:1], scalar1=-1.0,
                                          scalar2=rstd[:, q, 0:1], op0=ALU.mult, op1=ALU.mult))
            wait(A, m, dest_free)
            free["mv", q] = c_a.after(A.activation(dest, x[0:TN, t, :], ACT.Relu, bias=rstd[:, q, 1:2], scale=rstd[:, q, 0:1]))
            return free["mv", q]

        def transpose_rows(key, t, rows_ap, ready):
            q = t % 2
            wait(P, ready, free.get(("bankT", q)))
            for k in range(KB):
                last = P.transpose(bank[4 + q][:, k * TN:(k + 1) * TN], rows_ap[:, k * 128:(k + 1) * 128], ident[0:TN, 0:TN])
            marks[key, t] = c_p.after(last)

        def high_half(key, t, ready, relu=False):
            q = t % 2
            wait(A, ready, free.get(("hT", q)))
            marks[key, t] = c_a.after(A.activation(hTh[:, q, :, :].rearrange("p k n -> p (k n)"), bank[4 + q][:, 0:KB * TN],
                                                   ACT.Relu if relu else ACT.Copy))

        def low_half(key, t, ready, relu=False):
            q = t % 2
            b = bank[4 + q][:, 0:KB * TN]
            high = hTh[:, q, :, :].rearrange("p k n -> p (k n)").bitcast(F32)
            low = hTl[:, q, :, :].rearrange("p k n -> p (k n)")
            wait(V, ready)
            if relu:
                ins = V.scalar_tensor_tensor(out=low, in0=b, scalar=0.0, in1=high, op0=ALU.max, op1=ALU.subtract)
            else:
                ins = V.tensor_tensor(low, b, high, ALU.subtract)
            free["bankT", q] = marks[key, t] = c_v.after(ins)

        def product(out_ap, q, high, low):
            last = None
            for k in range(KB):
                for n, (a, b) in enumerate(((hTh, high), (hTh, low), (hTl, high))):
                    last = P.matmul(out_ap, a[:, q, k, :], b[:, k, :], start=(k == 0 and n == 0),
                                    stop=(k == KB - 1 and n == 2))
            return last

        def project(t, ready, high, low):
            q = t % 2
            wait(P, ready, free.get(("bankZ", q)))
            free["hT", q] = c_p.after(product(bank[6 + q][0:TN, :], q, high, low))
            return free["hT", q]

        def store(t, dest, rows_ap, ready):
            wait(S, ready)
            return c_st[t % 3].after(S.dma_start(dest[t * TN:(t + 1) * TN, :], rows_ap), 16)

        LOADED = 8
        tile_regs = {}

        def step_tile(engine, name, i):
            if (name, 0) not in tile_regs:
                for n in range(LOADED):
                    tile_regs[name, n] = engine.alloc_register(f"tile_{name}{n}")
            if i % LOADED == 0:
                engine.reg_load([tile_regs[name, n] for n in range(LOADED)], tile_row[0:1, i:i + LOADED])
            return nc.s_assert_within(engine.snap(tile_regs[name, i % LOADED]), 0, TILES - 1,
                                      skip_runtime_bounds_check_because="a count of TILES - 1 comparisons")

        done = {"pe": [], "acc": None}

        def aggregate(layer, target, weights, table_ready, target_ready, alpha=None, beside=None):
            base = len(done["pe"])
            sels, gathered, scaled, acc_marks = {}, {}, {}, {}
            wait(V, *target_ready)
            wait(G, *table_ready)

            def select(i):
                n = base + i
                if n >= SELS:
                    wait(V, done["pe"][n - SELS])
                if weights:
                    ins = V.tensor_scalar(out=sel[:, n % SELS, :], in0=node_iota[:, :], scalar1=dl_t[:, i:i + 1],
                                          scalar2=w_t[:, i:i + 1], op0=ALU.is_equal, op1=ALU.mult)
                else:
                    ins = V.tensor_scalar(out=sel[:, n % SELS, :], in0=node_iota[:, :], scalar1=dl_t[:, i:i + 1],
                                          scalar2=None, op0=ALU.is_equal)
                sels[i] = c_v.after(ins)

            def gather(i):
                n = base + i
                if n >= RING:
                    wait(G, done["pe"][n - RING])
                gathered[i] = c_ring[n % RING].after(G.indirect_dma_start(
                    out=ring[:, n % RING, :], out_offset=None, in_=table[layer][:, :],
                    in_offset=bass.IndirectOffsetOnAxis(ap=src_t[:, i:i + 1], axis=0)), 16)

            def scale(i):
                slot = ring[:, (base + i) % RING, :].rearrange("p (h j) -> p h j", h=H)
                wait(V, gathered[i])
                dve_part = c_v.after(V.tensor_tensor(slot[:, 0:HV, :], slot[:, 0:HV, :],
                                                     alpha[:, i, 0:HV, None].to_broadcast([CE, HV, DP]), ALU.mult))
                wait(A, gathered[i])
                for h in range(HV, H):
                    last = A.activation(slot[:, h, :], slot[:, h, :], ACT.Copy, scale=alpha[:, i, h:h + 1])
                scaled[i] = (dve_part, c_a.after(last))

            HV = 4
            for i in range(STEPS + AHEAD):
                j = i - AHEAD
                if i < STEPS:
                    gather(i)
                    select(i)
                if alpha is not None and 0 <= i - SCALE_AHEAD < STEPS:
                    scale(i - SCALE_AHEAD)
                if j < 0:
                    continue
                n = base + j
                wait(P, *(scaled[j] if alpha is not None else (gathered[j],)))
                wait(P, sels[j], acc_marks.get(j - NAGG))
                mark = c_p.after(P.matmul(bank[n % NAGG][0:TN, :], sel[:, n % SELS, :], ring[:, n % RING, :],
                                          start=True, stop=True))
                done["pe"].append(mark)
                t = step_tile(V, "v", j)
                wait(V, mark, done["acc"])
                part = target[0:TN, bass.ds(t, 1), :].rearrange("p a d -> p (a d)")
                done["acc"] = acc_marks[j] = c_v.after(V.tensor_tensor(part, part, bank[n % NAGG][0:TN, :], ALU.add))
                if beside is not None:
                    next(beside, None)
            if beside is not None:
                for _ in beside:
                    pass
            return done["acc"]

        def pipeline(stages, beside=None):
            for n in range(TILES + max(lag for lag, _ in stages)):
                for lag, stage_of in stages:
                    if 0 <= n - lag < TILES:
                        stage_of(n - lag)
                if beside is not None:
                    next(beside, None)
            if beside is not None:
                for _ in beside:
                    pass

        def last_stores(key):
            return [marks[key, t] for t in range(TILES - 3, TILES)]

        k_w0 = split_weight(wh, wl, flat_ring[:, 7 * D:11 * D].rearrange("p (k d) -> p k d", k=KB), k_w)
        wait(P, k_w0, k_ident)
        wait(A, k_const)

        def l0_stats(t):
            norm_stats(t, k_x[t // XQ])

        def l0_relu(t):
            wait(A, k_x[t // XQ])
            marks["h", t] = norm_relu(t, hbuf(t % 2), marks.get(("tr", t - 2)))

        def plain_tr(t):
            transpose_rows("tr", t, hbuf(t % 2), marks["h", t])

        def plain_high(t):
            high_half("hTh", t, marks["tr", t])

        def plain_low(t):
            low_half("hT", t, marks["hTh", t])

        def l0_mm(t):
            marks["z", t] = project(t, marks["hT", t], wh, wl)

        def l0_out(t):
            wait(A, marks["z", t], marks.get(("st", t - 3)))
            free["bankZ", t % 2] = m = c_a.after(A.copy(zbuf(t % 3), bank[6 + t % 2][0:TN, :]))
            marks["st", t] = store(t, table[0], zbuf(t % 3), m)
            wait(G, marks["hT", t])
            marks["zero", t] = c_g.after(G.memset(acc[0:TN, t, :], 0.0))

        pipeline([(3, plain_high), (1, l0_relu), (0, l0_stats), (5, l0_out), (3, plain_low), (4, l0_mm), (2, plain_tr)],
                 beside=step_tables())

        def beside_l0():
            yield from degrees()
            wait(S, marks["dis"])
            m = c_w.after(S.dma_start(raw_w, W1_in.rearrange("(k p) d -> p k d", p=128)), 16)
            k_b = c_w.after(S.dma_start(bias_bc[:, :], b1_in.rearrange("(a d) -> a d", a=1).to_broadcast([TN, D])), 16)
            for _ in range(8):
                yield
            wait(P, k_b)
            wait(V, k_b)
            for k in range(KB):
                wait(P, marks.get(("wsplit", k - 2)))
                for j in range(KB):
                    last = P.transpose(bank[5 + k % 2][:, j * 128:(j + 1) * 128], raw_w[:, j, k * 128:(k + 1) * 128], ident[:, :])
                m = marks["wread"] = c_p.after(last)
                yield
                marks["wsplit", k] = split(wh[:, k, :], wl[:, k, :], bank[5 + k % 2][:, :], m)
            wait(P, m, marks["wsplit", KB - 1])
            wait(A, marks["wread"])

        wait(V, marks["tables"], marks["zero", TILES - 1])
        wait(G, marks["tables"])
        wait(A, marks["masked"], *last_stores("st"))
        k_acc = aggregate(0, acc, True, last_stores("st"), last_stores("st"), beside=beside_l0())

        def l1_stats(t):
            m = c_v.after(V.scalar_tensor_tensor(out=x[0:TN, t, :], in0=acc[0:TN, t, :], scalar=0.0, in1=x[0:TN, t, :],
                                                 op0=ALU.max, op1=ALU.add))
            marks["xr", t] = m
            norm_stats(t, m)

        def l1_relu(t):
            wait(A, marks["xr", t])
            marks["h", t] = norm_relu(t, hbuf(t % 2), marks["tr", (t - 2) % TILES])

        def l1_out(t):
            wait(V, marks["z", t], marks.get(("scaled", t - 3)))
            free["bankZ", t % 2] = m = c_v.after(V.tensor_tensor(zbuf(t % 3), bank[6 + t % 2][0:TN, :], bias_bc[:, :], ALU.add))
            wait(A, m)
            marks["scaled", t] = m = c_a.after(A.activation(acc[0:TN, t, :], zbuf(t % 3), ACT.Copy, scale=dis[:, t:t + 1]))
            marks["st", t] = store(t, table[1], acc[0:TN, t, :], m)

        wait(V, k_acc)
        pipeline([(3, plain_high), (1, l1_relu), (0, l1_stats), (5, l1_out), (3, plain_low), (4, l0_mm), (2, plain_tr)])
        b2_bc = stage[0:TN, 4 * D:5 * D]

        def beside_l1():
            wait(S, marks["scaled", TILES - 1], marks["hT", TILES - 1], marks["z", TILES - 1])
            m = c_w.after(S.dma_start(raw_w, G1_in.rearrange("(k p) d -> p k d", p=128)), 16)
            for _ in range(12):
                yield
            for k in range(KB):
                marks["g1w"] = split(wh[:, k, :], wl[:, k, :], raw_w[:, k, :], m)
                yield
            wait(S, marks["g1w"])
            c_w2.after(S.dma_start(bias_bc[:, :], g1_in.rearrange("(a d) -> a d", a=1).to_broadcast([TN, D])), 16)
            marks["biases"] = c_w2.after(S.dma_start(b2_bc, g2_in.rearrange("(a d) -> a d", a=1).to_broadcast([TN, D])), 16)
            wait(A, marks["g1w"])
            wait(V, marks["biases"])

        k_acc = aggregate(1, acc, False, last_stores("st"), last_stores("st"), beside=beside_l1())

        wait(A, k_acc)

        def l2_sum(t):
            wait(A, marks.get(("xadd", t - 2)))
            marks["r2", t] = c_a.after(A.activation(hbuf(t % 2), acc[0:TN, t, :], ACT.Relu, scale=dis[:, t:t + 1]))

        def l2_stats(t):
            wait(V, marks["r2", t])
            marks["xadd", t] = c_v.after(V.tensor_tensor(x[0:TN, t, :], x[0:TN, t, :], hbuf(t % 2), ALU.add))
            norm_stats(t, marks["xadd", t])

        def l2_relu(t):
            wait(A, marks["xadd", t])
            m = marks["h2", t] = norm_relu(t, acc[0:TN, t, :])
            marks["st", t] = store(t, table[2], acc[0:TN, t, :], m)

        pipeline([(0, l2_sum), (2, l2_relu), (1, l2_stats)])

        FW = RB * CE
        keep, nlast, pf, pb_ = (big[0:RS, n * FW:(n + 1) * FW].rearrange("p (b e) -> p b e", b=RB) for n in range(4))
        row8 = stage[0:H, 0:4 * (STEPS + 2)].rearrange("p (a i) -> p a i", a=4)
        r8x = stage[0:H, 4 * (STEPS + 2):4 * (STEPS + 2) + STEPS]
        zero = sb("zero", [RS, CE])

        def to_row8(lane_of_edge8, row, shift, b, bk, ready, free_mark):
            wait(P, ready, free_mark)
            m = c_p.after(P.transpose(bank[bk][0:H, 0:RS], edge8[:, b, lane_of_edge8, :], ident[0:RS, 0:RS]))
            wait(V, m)
            return c_v.after(V.tensor_copy(row8[:, row, shift + b * RS:shift + (b + 1) * RS], bank[bk][0:H, 0:RS]))

        def to_back8(row_ap, lane, b, bk, ready, free_mark):
            wait(P, ready, free_mark)
            m = c_p.after(P.transpose(bank[bk][0:RS, 0:H], row_ap, ident[0:H, 0:H]))
            wait(V, m)
            return c_v.after(V.tensor_copy(back8[:, b, lane, :], bank[bk][0:RS, 0:H]))

        def beside_l2():
            for t in range(TILES):
                m = c_v.after(V.tensor_tensor(x[0:TN, t, :], x[0:TN, t, :], b2_bc, ALU.add))
                yield
                yield
                yield
            c_v.after(V.tensor_tensor(keep[:, :, 1:CE], dstf[:, :, 1:CE], dstf[:, :, 0:CE - 1], ALU.is_equal))
            c_v.after(V.tensor_copy(edge8[:, :, 0, :], dstf[:, :, 0:1].to_broadcast([RS, RB, H])))
            c_v.after(V.tensor_copy(edge8[:, :, 1, :], dstf[:, :, CE - 1:CE].to_broadcast([RS, RB, H])))
            c_v.after(V.memset(zero[:, :], 0.0))
            wait(V, m)
            m = c_v.after(V.memset(row8, -1.0))
            wait(V, m)
            last = None
            for b in range(RB):
                for s in range(2):
                    last = to_row8(s, s, 1 + s, b, 4, m, last)
                    yield
            wait(V, last)
            m = c_v.after(V.memset(row8[:, 2, :], 0.0))
            wait(V, m)
            m = last = c_v.after(V.tensor_tensor(row8[:, 2, 1:STEPS + 1], row8[:, 0, 1:STEPS + 1], row8[:, 1, 1:STEPS + 1],
                                                 ALU.is_equal))
            for b in range(RB):
                for lane in range(2):
                    last = to_back8(row8[:, 2, 1 + lane + b * RS:1 + lane + (b + 1) * RS], lane, b, 4, m, last)
                    yield
            wait(V, last)
            c_v.after(V.tensor_copy(keep[:, :, 0:1], back8[:, :, 0, 0:1]))
            m = c_v.after(V.tensor_copy(nlast[:, :, CE - 1:CE], back8[:, :, 1, 0:1]))
            wait(V, m)
            m = c_v.after(V.tensor_copy(nlast[:, :, 0:CE - 1], keep[:, :, 1:CE]))
            wait(V, m)
            for b in range(RB):
                c_v.after(V.tensor_tensor_scan(pf[:, b, :], keep[:, b, :], zero[:, :], 1.0, ALU.mult, ALU.add))
                yield
                m = c_v.after(V.tensor_tensor_scan(pb_[:, b, ::-1], nlast[:, b, ::-1], zero[:, :], 1.0, ALU.mult, ALU.add))
                yield
            wait(V, m)
            c_v.after(V.tensor_copy(edge8[:, :, 0, :], pf[:, :, CE - 1:CE].to_broadcast([RS, RB, H])))
            m = c_v.after(V.tensor_copy(edge8[:, :, 1, :], pb_[:, :, 0:1].to_broadcast([RS, RB, H])))
            last = None
            for b in range(RB):
                for s in range(2):
                    last = to_row8(s, 2 + s, 1, b, 4, m, last)
                    yield
            free["bankT", 0] = last
            wait(V, last)
            marks["flags"] = c_v.after(V.tensor_copy(flags8[:, :, :], row8[:, 2:4, 1:STEPS + 1]))
            wait(V, marks["flags"])
            wait(A, marks["flags"])

        flags8 = sb("flags8", [H, 2, STEPS])
        k_acc = aggregate(2, acc, False, last_stores("st"), last_stores("st"), beside=beside_l2())

        raw2 = flat_ring[:, 0:KB * D].rearrange("p (k d) -> p k d", k=KB)
        raw3 = flat_ring[:, KB * D:2 * KB * D].rearrange("p (k d) -> p k d", k=KB)
        raw3h = flat_ring[:, KB * D:2 * KB * D].rearrange("p (k h j) -> p k h j", k=KB, h=H)
        aw_bc = flat_ring[:, 2 * KB * D:(2 * KB + 2) * D].rearrange("p (s h j) -> p s h j", s=2, h=H)
        wb_bc = flat_ring[0:TN, (2 * KB + 2) * D:(2 * KB + 3) * D]
        wait(S, done["pe"][-1])
        k_w2 = c_w2.after(S.dma_start(raw2, G2_in.rearrange("(k p) d -> p k d", p=128)), 16)
        for k in range(KB):
            c_w.after(S.dma_start(raw3h[:, k, :, :], Ws_in[:, k * 128:(k + 1) * 128, :].rearrange("h p j -> p h j")), 16)
        for s in range(2):
            c_w.after(S.dma_start(aw_bc[:, s, :, :], aw_in[:, s * DP:(s + 1) * DP].rearrange("(a h) j -> a h j", a=1)
                                  .to_broadcast([128, H, DP])), 16)
        c_w.after(S.dma_start(wb_bc, Wb_in.rearrange("(a h) j -> a (h j)", a=1).to_broadcast([TN, D])), 16)
        k_w3 = c_w.after(S.dma_start(ab_bc[:, :], ab_in.rearrange("(a h) -> a h", a=1).to_broadcast([TN, H])), 16)

        def score_weights():
            prod = flat_ring[:, (2 * KB + 3) * D:(2 * KB + 4) * D].rearrange("p (h j) -> p h j", h=H)
            yield
            yield
            yield
            wait(V, k_w3)
            m = None
            for s in range(2):
                for k in range(KB + 1):
                    wait(V, m)
                    if k < KB:
                        m = c_v.after(V.tensor_tensor(prod, raw3h[:, k, :, :], aw_bc[:, s, :, :], ALU.mult))
                        wait(V, m)
                        m = c_v.after(V.tensor_reduce(wa[:, k, s * H:(s + 1) * H], prod, axis=AX.X, op=ALU.add))
                    else:
                        m = c_v.after(V.tensor_tensor(prod[0:TN], wb_bc.rearrange("p (h j) -> p h j", h=H), aw_bc[0:TN, s, :, :], ALU.mult))
                        wait(V, m)
                        m = c_v.after(V.tensor_reduce(sc_bias[:, s * H:(s + 1) * H], prod[0:TN], axis=AX.X, op=ALU.add))
                    yield
            wait(V, m)
            m = c_v.after(V.tensor_tensor(sc_bias[:, 0:H], sc_bias[:, 0:H], ab_bc[:, :], ALU.add))
            marks["wa"] = m

        wait(P, k_acc)
        free["hT", 0] = free["hT", 1] = None

        def g_tr(t):
            transpose_rows("gtr", t, acc[0:TN, t, :], None)

        def g_high(t):
            high_half("g1h", t, marks["gtr", t])

        def g_low(t):
            low_half("g1T", t, marks["g1h", t])

        def g_mm1(t):
            marks["g1", t] = project(t, marks["g1T", t], wh, wl)

        def g_bias(t):
            wait(V, marks["g1", t], marks["gtr", t])
            free["bankZ", t % 2] = marks["z1", t] = c_v.after(V.tensor_tensor(
                acc[0:TN, t, :], bank[6 + t % 2][0:TN, :], bias_bc[:, :], ALU.add))

        pipeline([(1, g_high), (3, g_bias), (1, g_low), (2, g_mm1), (0, g_tr)], beside=score_weights())

        wait(A, marks["g1", TILES - 1])
        wait(V, marks["g1", TILES - 1])
        k_w = split_weight(wh, wl, raw2, k_w2)
        wait(P, k_w, marks["wa"])
        hT3 = flat_ring[:, 2 * KB * D:2 * KB * D + 2 * KB * TN].rearrange("p (q k n) -> p q k n", q=2, k=KB)
        wait(A, marks["wa"])

        def g_tr2(t):
            transpose_rows("gtr2", t, acc[0:TN, t, :], marks["z1", t])

        def g_high2(t):
            high_half("g2h", t, marks["gtr2", t], relu=True)

        def g_low2(t):
            low_half("g2T", t, marks["g2h", t], relu=True)

        def g_mm2(t):
            marks["g2", t] = project(t, marks["g2T", t], wh, wl)

        def g_add(t):
            wait(V, marks["g2", t])
            free["bankZ", t % 2] = marks["x", t] = c_v.after(V.tensor_tensor(x[0:TN, t, :], x[0:TN, t, :],
                                                                             bank[6 + t % 2][0:TN, :], ALU.add))
            norm_stats(t, marks["x", t])

        def l3_relu(t):
            wait(A, marks["x", t])
            marks["h", t] = norm_relu(t, acc[0:TN, t, :], marks["gtr2", t])

        def s_tr(t):
            wait(P, marks["h", t], marks.get(("hT3", t - 2)))
            for k in range(KB):
                last = P.transpose(bank[2 + t % 2][:, k * TN:(k + 1) * TN], acc[0:TN, t, k * 128:(k + 1) * 128], ident[0:TN, 0:TN])
            marks["str", t] = c_p.after(last)

        def s_copy(t):
            wait(A, marks["str", t], marks.get(("s", t - 2)))
            marks["hT3", t] = c_a.after(A.copy(hT3[:, t % 2, :, :].rearrange("p k n -> p (k n)"), bank[2 + t % 2][:, 0:KB * TN]))

        def s_mm(t):
            wait(P, marks["hT3", t], marks.get(("sc", t - 2)))
            for k in range(KB):
                last = P.matmul(bank[t % 2][0:TN, 0:2 * H], hT3[:, t % 2, k, :], wa[:, k, :], start=(k == 0), stop=(k == KB - 1))
            marks["s", t] = c_p.after(last)

        def s_out(t):
            q = t % 2
            wait(V, marks["s", t], marks.get(("us", t - 2)))
            c_v.after(V.tensor_tensor(t_all[:, t, :], bank[q][0:TN, 0:H], sc_bias[:, 0:H], ALU.add))
            m = marks["sc", t] = c_v.after(V.tensor_tensor(u_out[:, q, :], bank[q][0:TN, H:2 * H], sc_bias[:, H:2 * H], ALU.add))
            wait(S, m)
            marks["us", t] = c_us[q].after(S.dma_start(score_table[t * TN:(t + 1) * TN, :], u_out[:, q, :]), 16)

        pipeline([(1, g_high2), (6, s_copy), (4, l3_relu), (3, g_add), (1, g_low2), (8, s_out),
                  (2, g_mm2), (0, g_tr2), (5, s_tr), (7, s_mm)])
        stored_u = [marks["us", t] for t in range(TILES - 2, TILES)]

        wait(A, marks["g2", TILES - 1])
        wait(V, marks["g2", TILES - 1])
        k_w = split_weight(wh, wl, raw3, k_w3)
        wait(P, k_w)

        def l3_tr(t):
            transpose_rows("tr3", t, acc[0:TN, t, :], marks["h", t])

        def l3_high(t):
            high_half("h3h", t, marks["tr3", t])

        def l3_low(t):
            low_half("h3T", t, marks["h3h", t])

        def l3_mm(t):
            marks["z3", t] = project(t, marks["h3T", t], wh, wl)

        def l3_out(t):
            wait(V, marks["z3", t], marks.get(("st3", t - 3)))
            m = free["bankZ", t % 2] = c_v.after(V.tensor_tensor(zbuf(t % 3), bank[6 + t % 2][0:TN, :], wb_bc, ALU.add))
            marks["st3", t] = store(t, table[3], zbuf(t % 3), m)

        pipeline([(1, l3_high), (3, l3_out), (1, l3_low), (2, l3_mm), (0, l3_tr)])
        stored = last_stores("st3")

        ue = big[:, 4 * FW:4 * FW + STEPS * H].rearrange("p (i h) -> p i h", h=H)
        te = flat_ring[:, 0:STEPS * H].rearrange("p (i h) -> p i h", h=H)
        kbig, pfb, lastf = (flat_ring[0:RS, (8 + n) * FW:(9 + n) * FW].rearrange("p (b e) -> p b e", b=RB) for n in range(3))
        selT = flat_ring[0:TN, 11 * FW:11 * FW + 4 * CE].rearrange("p (a b) -> p a b", b=CE)
        ex = flat_ring[0:RS, 0:RB * H * CE].rearrange("p (b h e) -> p b h e", b=RB, h=H)
        flat_acc = acc[:, :, :].rearrange("p a b -> p (a b)")
        WR = RB * H * CE
        zr, fr = (flat_acc[0:RS, n * WR:(n + 1) * WR].rearrange("p (b h e) -> p b h e", b=RB, h=H) for n in range(2))

        def wide(v):
            return v.rearrange("p b h e -> p (b h e)")

        wait(G, *stored_u, marks["flags"])
        k_ue = []
        for b in range(RB):
            for i in range(b * RS, (b + 1) * RS):
                m = c_ue[b].after(G.indirect_dma_start(out=ue[:, i, :], out_offset=None, in_=score_table[:, :],
                                                       in_offset=bass.IndirectOffsetOnAxis(ap=src_t[:, i:i + 1], axis=0)), 16)
            k_ue.append(m)

        wait(V, marks["z3", TILES - 1], *stored)
        wait(A, *stored)
        c_v.after(V.tensor_scalar(out=lastf, in0=nlast, scalar1=-1.0, scalar2=1.0, op0=ALU.mult, op1=ALU.add))
        c_v.after(V.tensor_scalar(out=kbig, in0=keep, scalar1=-1.0, scalar2=BIG, op0=ALU.add, op1=ALU.mult))
        m = c_v.after(V.tensor_scalar(out=pfb, in0=pf, scalar1=-1.0, scalar2=BIG, op0=ALU.add, op1=ALU.mult))
        wait(V, m)
        wait(P, m, marks["sc", TILES - 1], free["bankT", 0], free["bankT", 1], free["bankZ", 0], free["bankZ", 1])
        wait(A, m)
        tb = {}
        n_te = 0

        def target_scores(b):
            for i in range(b * RS, (b + 1) * RS):
                q = i % 4
                wait(V, tb.get(("tr", i - 4)))
                m = c_v.after(V.tensor_scalar(out=sel[:, q, :], in0=node_iota[:, :], scalar1=dl_t[:, i:i + 1],
                                              scalar2=None, op0=ALU.is_equal))
                wait(P, m, tb.get(("cp", i - 4)))
                m = tb["tr", i] = c_p.after(P.transpose(bank[2 + q][0:TN, 0:CE], sel[:, q, :], ident[:, :]))
                wait(A, m, tb.get(("te", i - 4)))
                tb["cp", i] = c_a.after(A.copy(selT[:, q, :], bank[2 + q][0:TN, 0:CE]))
                if i >= b * RS + 3:
                    target_product(b, i - 3)
            for i in range((b + 1) * RS - 3, (b + 1) * RS):
                target_product(b, i)
            wait(V, tb["te", (b + 1) * RS - 1])
            tb["teb", b] = c_v.after(V.tensor_copy(te[:, b * RS:(b + 1) * RS, :].rearrange("p i h -> p (i h)")[:, 0:RS * H // 2],
                                                   bank[0][:, 0:RS * H // 2]))
            tb["teb", b] = c_v.after(V.tensor_copy(te[:, b * RS:(b + 1) * RS, :].rearrange("p i h -> p (i h)")[:, RS * H // 2:RS * H],
                                                   bank[1][:, 0:RS * H // 2]))

        def target_product(b, i):
            t = step_tile(P, "p", i)
            j = i - b * RS
            wait(P, tb["cp", i])
            if j == 0:
                wait(P, tb.get(("teb", b - 1)))
            bk, jj = (0, j) if j < RS // 2 else (1, j - RS // 2)
            tb["te", i] = c_p.after(P.matmul(bank[bk][:, jj * H:(jj + 1) * H], selT[:, i % 4, :],
                                             t_all[:, bass.ds(t, 1), :].rearrange("p a h -> p (a h)"), start=True, stop=True))

        def edge_scores(b):
            for half in range(2):
                h0 = half * 4
                wait(P, k_ue[b], tb["teb", b], tb.get(("bu", 0)), tb.get(("bt", 0)))
                for j in range(4):
                    last = P.transpose(bank[6][0:RS, j * CE:(j + 1) * CE], ue[:, b * RS:(b + 1) * RS, h0 + j], ident[:, :])
                for j in range(4):
                    last = P.transpose(bank[7][0:RS, j * CE:(j + 1) * CE], te[:, b * RS:(b + 1) * RS, h0 + j], ident[:, :])
                m = c_p.after(last)
                z = zr[:, b, h0:h0 + 4, :]
                zf = z.rearrange("p h e -> p (h e)")
                wait(A, m)
                m = tb["bu", 0] = c_a.after(A.copy(zf, bank[6][0:RS, :]))
                wait(V, m)
                m = tb["bt", 0] = c_v.after(V.tensor_tensor(zf, zf, bank[7][0:RS, :], ALU.add))
                wait(V, m)
                m = c_v.after(V.scalar_tensor_tensor(out=zf, in0=zf, scalar=SLOPE, in1=zf, op0=ALU.mult, op1=ALU.max))
                wait(V, m)
                m = c_v.after(V.tensor_tensor(z, z, masked[:, b, None, :].to_broadcast([RS, 4, CE]), ALU.add))
                wait(V, m)
                for h in range(h0, h0 + 4):
                    tb["fr", b] = c_v.after(V.tensor_tensor_scan(fr[:, b, h, :], kbig[:, b, :], zr[:, b, h, :], -BIG, ALU.add, ALU.max))

        for b in range(RB):
            target_scores(b)
            if b:
                edge_scores(b - 1)
        edge_scores(RB - 1)

        def hand_on(column, reverse, sums, lane, ready):
            wait(V, ready)
            for b in range(RB):
                m = c_v.after(V.tensor_copy(edge8[:, b, 0, :], column(b)))
            wait(P, m, ready)
            for b in range(RB):
                last = P.transpose(bank[4][0:H, b * RS:(b + 1) * RS], edge8[:, b, 0, :], ident[0:RS, 0:RS])
            m = c_p.after(last)
            wait(V, m)
            m = c_v.after(V.tensor_copy(row8[:, 0, 0:STEPS], bank[4][0:H, 0:STEPS]))
            wait(V, m)
            if reverse:
                c_v.after(V.memset(r8x[:, STEPS - 1:STEPS], 0.0))
                m = c_v.after(V.tensor_tensor_scan(r8x[:, 0:STEPS - 1][:, ::-1], flags8[:, 1, 1:STEPS][:, ::-1],
                                                   row8[:, 0, 1:STEPS][:, ::-1], 0.0, ALU.mult, ALU.add))
            elif sums:
                c_v.after(V.memset(r8x[:, 0:1], 0.0))
                m = c_v.after(V.tensor_tensor_scan(r8x[:, 1:STEPS], flags8[:, 0, 0:STEPS - 1],
                                                   row8[:, 0, 0:STEPS - 1], 0.0, ALU.mult, ALU.add))
            else:
                m = c_v.after(V.tensor_scalar(out=row8[:, 1, 0:STEPS], in0=flags8[:, 0, :], scalar1=-1.0, scalar2=BIG,
                                              op0=ALU.add, op1=ALU.mult))
                c_v.after(V.memset(r8x[:, 0:1], -BIG))
                wait(V, m)
                m = c_v.after(V.tensor_tensor_scan(r8x[:, 1:STEPS], row8[:, 1, 0:STEPS - 1],
                                                   row8[:, 0, 0:STEPS - 1], -BIG, ALU.add, ALU.max))
            wait(P, m)
            for b in range(RB):
                last = P.transpose(bank[5][0:RS, b * H:(b + 1) * H], r8x[:, b * RS:(b + 1) * RS], ident[0:H, 0:H])
            m = c_p.after(last)
            wait(V, m)
            m = c_v.after(V.tensor_copy(back8[:, :, lane, :], bank[5][0:RS, 0:RB * H].rearrange("p (b h) -> p b h", b=RB)))
            wait(V, m)

        def segment_total(data, sums, ready):
            hand_on(lambda b: fr[:, b, :, CE - 1], False, sums, 0, ready)
            for b in range(RB):
                for h in range(H):
                    m = c_v.after(V.scalar_tensor_tensor(
                        out=fr[:, b, h, :], in0=(pf if sums else pfb)[:, b, :], scalar=back8[:, b, 0, h:h + 1],
                        in1=fr[:, b, h, :], op0=ALU.mult if sums else ALU.add, op1=ALU.add if sums else ALU.max))
                wait(V, m)
                m = c_v.after(V.tensor_tensor(fr[:, b, :, :], fr[:, b, :, :], lastf[:, b, None, :].to_broadcast([RS, H, CE]), ALU.mult))
                wait(V, m)
                for h in range(H):
                    m = c_v.after(V.tensor_tensor_scan(data[:, b, h, ::-1], nlast[:, b, ::-1], fr[:, b, h, ::-1], 0.0, ALU.mult, ALU.add))
            hand_on(lambda b: data[:, b, :, 0], True, sums, 1, m)
            for b in range(RB):
                for h in range(H):
                    m = c_v.after(V.scalar_tensor_tensor(out=data[:, b, h, :], in0=pb_[:, b, :], scalar=back8[:, b, 1, h:h + 1],
                                                         in1=data[:, b, h, :], op0=ALU.mult, op1=ALU.add))
                yield b, m

        mx = flat_acc[0:RS, 2 * WR:3 * WR].rearrange("p (b h e) -> p b h e", b=RB, h=H)
        for b, m in segment_total(mx, False, tb["fr", RB - 1]):
            wait(V, m)
            m = c_v.after(V.tensor_tensor(ex[:, b, :, :], zr[:, b, :, :], mx[:, b, :, :], ALU.subtract))
            wait(A, m)
            m = c_a.after(A.activation(ex[:, b, :, :], ex[:, b, :, :], ACT.Exp))
            tb["ex", b] = m
        for b in range(RB):
            wait(V, tb["ex", b])
            for h in range(H):
                m = c_v.after(V.tensor_tensor_scan(fr[:, b, h, :], keep[:, b, :], ex[:, b, h, :], 0.0, ALU.mult, ALU.add))
        alpha = ue
        prev = None
        for b, m in segment_total(mx, True, m):
            wait(V, m)
            m = c_v.after(V.reciprocal(mx[:, b, :, :], mx[:, b, :, :]))
            wait(V, m)
            m = c_v.after(V.tensor_tensor(mx[:, b, :, :], mx[:, b, :, :], ex[:, b, :, :], ALU.mult))
            for half in range(2):
                wait(P, m, tb.get(("al", half)))
                for j in range(4):
                    last = P.transpose(bank[6 + half][:, j * RS:(j + 1) * RS], mx[:, b, half * 4 + j, :], ident[0:RS, 0:RS])
                mm = c_p.after(last)
                wait(A, mm)
                tb["al", half] = c_a.after(A.copy(alpha[:, b * RS:(b + 1) * RS, half * 4:half * 4 + 4].rearrange("p i h -> p h i"),
                                                  bank[6 + half][:, 0:4 * RS].rearrange("p (h i) -> p h i", h=4)))
        wait(V, tb["al", 0], tb["al", 1])
        wait(A, tb["al", 0], tb["al", 1])
        wait(G, m, *stored)
        aggregate(3, x, False, [], [], alpha=alpha)
        wait(S, done["acc"])
        for q in range(5):
            k_out = c_out[q].after(S.dma_start(out[q * XQ * TN:(q + 1) * XQ * TN, :].rearrange("(t p) d -> p t d", p=TN),
                                               x[0:TN, q * XQ:(q + 1) * XQ, :]), 16)
        for q in range(5):
            wait(S, (c_out[q].sem, c_out[q].value))


INPUTS = ["x", "src", "dst", "edge_weight", "L0_gnn_W", "L1_gnn_W", "L1_gnn_b", "L2_gnn_W1", "L2_gnn_b1",
          "L2_gnn_W2", "L2_gnn_b2", "L3_gnn_Ws", "L3_gnn_Wb", "L3_gnn_a_w", "L3_gnn_a_b"]


def kernel(**inputs):
    import concourse.bacc as bacc
    from concourse.bass_utils import run_bass_kernel_spmd as run

    nc = bacc.Bacc("TRN2", target_bir_lowering=False, num_devices=1)
    arrays, args = {}, []
    for name in INPUTS:
        a = np.ascontiguousarray(inputs[name])
        arrays["in_" + name] = a
        args.append(nc.dram_tensor("in_" + name, a.shape, mybir.dt.from_np(a.dtype), kind="ExternalInput").ap())
    result = nc.dram_tensor("out_0", inputs["x"].shape, F32, kind="ExternalOutput").ap()
    build(nc, *args, result)
    r = run(nc, [arrays], core_ids=[0])
    return r.results[0]["out_0"]
```

```python
import numpy as np
import concourse.bass as bass
from concourse import mybir
from contextlib import ExitStack

F32 = mybir.dt.float32
I32 = mybir.dt.int32
F32R = mybir.dt.float32r
BF16 = mybir.dt.bfloat16
ALU = mybir.AluOpType
ACT = mybir.ActivationFunctionType
AX = mybir.AxisListType


class Count:

    def __init__(self, sem):
        self.sem, self.value = sem, 0

    def after(self, instruction, by=1):
        instruction.then_inc(self.sem, by)
        self.value += by
        return (self.sem, self.value)


def build(nc, x_in, src_in, dst_in, w_in, W0_in, W1_in, b1_in, G1_in, g1_in, G2_in, g2_in,
          Ws_in, Wb_in, aw_in, ab_in, out):
    N, D = x_in.shape
    E = src_in.shape[0]
    H, _, DP = Ws_in.shape
    TN = 125
    TILES = N // TN
    CE = 128
    CHUNKS = -(-E // CE)
    STEPS = CHUNKS + TILES - 1
    RB = 4
    RS = STEPS // RB
    KB = D // 128
    EC = 4
    EP = CHUNKS // EC
    EROW = EC * CE
    RING = 12
    SELS = 8
    AHEAD = 4
    SCALE_AHEAD = 2
    SB = 4
    NAGG = 4
    EPS = 1e-5
    BIG = 1e30
    FAR = 1 << 20
    UG = 8
    NG = STEPS // UG
    PG = 33
    US = (NG - PG) * UG
    TC = 20
    TP = 7
    SCORES_AFTER = {7: 0, 17: 1, 21: 2}
    SLOPE = 0.2
    assert STEPS % SB == 0 and SELS % SB == 0 and STEPS % SELS == 0
    assert KB * D == 2 * H * CE and NG * UG == STEPS and STEPS % TC == 0 and TC * 3 * H <= 512 and US % 2 == 0 and US // 2 <= 128
    assert TILES * TN == N and RB * RS == STEPS and EP * EC == CHUNKS and KB * 128 == D and H * DP == D

    ctx = ExitStack()
    with ctx:
        def sb(name, shape, dt=F32):
            return ctx.enter_context(nc.sbuf_tensor(name, shape, dt))

        def count(name):
            return Count(ctx.enter_context(nc.semaphore(name)))

        V, A, P, G, S = nc.vector, nc.scalar, nc.tensor, nc.gpsimd, nc.sync

        def wait(engine, *marks):
            for mark in marks:
                if mark is not None:
                    engine.wait_ge(*mark)

        edge_rows = nc.dram_tensor("edge_rows", (CHUNKS, 3 * CE), I32, kind="Internal").ap()
        table = [nc.dram_tensor(f"table{n}", (N, D), F32, kind="Internal").ap() for n in range(4)]
        dst_places = nc.dram_tensor("dst_places", (STEPS, CE), BF16, kind="Internal").ap()
        src_places = nc.dram_tensor("src_places", (US, CE), BF16, kind="Internal").ap()
        score_table = nc.dram_tensor("score_table", (N, H), F32, kind="Internal").ap()

        x = sb("x", [128, TILES, D])
        acc = sb("acc", [128, TILES, D])
        ring = sb("ring", [CE, RING, D])
        big = sb("big", [128, 5632])
        stage = sb("stage", [128, 5 * D])
        sel = sb("sel", [CE, SELS, TN])
        wh = sb("wh", [128, KB, D], F32R)
        wl = sb("wl", [128, KB, D], F32R)
        hTh = sb("hTh", [128, 2, KB, TN], F32R)
        hTl = sb("hTl", [128, 2, KB, TN], F32R)
        ident = sb("ident", [128, 128])
        node_iota = sb("node_iota", [128, TN])
        ones = sb("ones", [128, 128])
        eps = sb("eps", [128, 1])
        src_t = sb("src_t", [CE, STEPS], I32)
        dl_t = sb("dl_t", [CE, STEPS])
        w_t = sb("w_t", [CE, STEPS])
        tile_row = sb("tile_row", [1, STEPS], I32)
        dstf = sb("dstf", [RS, RB, CE])
        masked = sb("masked", [RS, RB, CE])
        dis = sb("dis", [TN, TILES])
        stats = sb("stats", [TN, 4, 6])
        mv = sb("mv", [TN, 4, 2])
        rstd = sb("rstd", [TN, 4, 2])
        bias_bc = sb("bias_bc", [TN, D])
        wa = sb("wa", [128, KB, 2 * H])
        u_all = sb("u_all", [TN, TILES, H])
        src_tile = sb("src_tile", [CE, US])
        place = sb("place", [128, 2])
        sc_bias = sb("sc_bias", [TN, 2 * H])
        ab_bc = sb("ab_bc", [TN, H])
        t_all = sb("t_all", [TN, TILES, H])
        edge8 = sb("edge8", [RS, RB, 2, H])
        back8 = sb("back8", [RS, RB, 2, H])

        flat_ring = ring[:, :, :].rearrange("p a b -> p (a b)")

        def hbuf(q):
            return stage[0:TN, q * D:(q + 1) * D]

        def zbuf(q):
            return stage[0:TN, (2 + q) * D:(3 + q) * D]

        raw_w = stage[:, 0:KB * D].rearrange("p (k d) -> p k d", k=KB)

        bank = [ctx.enter_context(nc.psum_tensor(f"bank{n}", [128, 512], F32)) for n in range(8)]

        c_v, c_a, c_p, c_g = count("c_v"), count("c_a"), count("c_p"), count("c_g")
        c_ld = count("c_ld")
        c_lx = count("c_lx")
        c_er = count("c_er")
        c_pt = count("c_pt")
        c_w = count("c_w")
        c_w2 = count("c_w2")
        c_st = [count(f"c_st{n}") for n in range(3)]
        c_dpl, c_spl = count("c_dpl"), count("c_spl")
        c_dp = [count(f"c_dp{n}") for n in range(2)]
        c_sp = [count(f"c_sp{n}") for n in range(2)]
        c_us = [count(f"c_us{n}") for n in range(2)]
        c_ring = [count(f"c_ring{n}") for n in range(RING)]
        c_ue = [count(f"c_ue{n}") for n in range(RB)]
        c_out = [count(f"c_out{n}") for n in range(5)]

        m = c_g.after(G.memset(ident[:, :], 0.0))
        wait(G, m)
        k_ident = c_g.after(G.affine_select(out=ident[:, :], in_=ident[:, :], compare_op=ALU.not_equal,
                                            fill=1.0, base=0, pattern=[[-1, 128]], channel_multiplier=1))
        iota_i = sb("iota_i", [128, TN], I32)
        m = c_g.after(G.iota(iota_i[:, :], pattern=[[1, TN]], base=0, channel_multiplier=0))
        step_i = sb("step_i", [RS, RB], I32)
        step_f = sb("step_f", [RS, RB])
        c_g.after(G.iota(step_i[:, :], pattern=[[RS, RB]], base=0, channel_multiplier=1))
        place_i = sb("place_i", [128, 1], I32)
        c_g.after(G.iota(place_i[:, :], pattern=[[0, 1]], base=0, channel_multiplier=1))
        tile_i = sb("tile_i", [128, TILES - 1], I32)
        tile_f = sb("tile_f", [128, TILES - 1])
        k_iota = c_g.after(G.iota(tile_i[:, :], pattern=[[CE, TILES - 1]], base=CE, channel_multiplier=0))

        ed = flat_ring[0:EP, 0:3 * D].bitcast(I32).rearrange("p (c a e) -> p c a e", c=EC, a=3)
        edf = flat_ring[0:EP, 0:3 * D].rearrange("p (c a e) -> p c a e", c=EC, a=3)
        k_x = []
        XQ = TILES // 5

        def load_x(engine, q):
            k_x.append(count(f"c_lx{q}").after(engine.dma_start(
                x[0:TN, q * XQ:(q + 1) * XQ, :],
                x_in[q * XQ * TN:(q + 1) * XQ * TN, :].rearrange("(t p) d -> p t d", p=TN)), 16))

        load_x(A, 0)
        k_w = c_w.after(A.dma_start(flat_ring[:, 7 * D:11 * D].rearrange("p (k d) -> p k d", k=KB),
                                    W0_in.rearrange("(k p) d -> p k d", p=128)), 16)
        for a, value in ((0, 0), (1, FAR), (2, 0)):
            k_pad = c_v.after(V.memset(ed[:, :, a, :], value))
        wait(S, k_pad)
        full = E // EROW
        rest = E - full * EROW
        rc = rest // CE
        for a, arr in enumerate((src_in, dst_in, w_in)):
            e = edf if a == 2 else ed
            k_ed = c_ld.after(S.dma_start(e[0:full, :, a, :], arr[0:full * EROW].rearrange(
                "(p c e) -> p c e", c=EC, e=CE)), 16)
            if rc:
                k_ed = c_ld.after(S.dma_start(e[full:full + 1, 0:rc, a, :], arr[full * EROW:full * EROW + rc * CE]
                                              .rearrange("(p c e) -> p c e", p=1, e=CE)), 16)
            if rest % CE:
                k_ed = c_ld.after(S.dma_start(e[full:full + 1, rc, a, 0:rest % CE],
                                              arr[full * EROW + rc * CE:E].rearrange("(p e) -> p e", p=1)), 16)
        for q in range(1, 5):
            load_x(S, q)
        wait(S, k_ed)
        k_er = c_er.after(S.dma_start(edge_rows.rearrange("(p c) e -> p (c e)", c=EC),
                                      ed.rearrange("p c a e -> p (c a e)")), 16)
        wait(V, k_iota)
        c_v.after(V.tensor_copy(node_iota[:, :], iota_i[:, :]))
        c_v.after(V.tensor_copy(step_f[:, :], step_i[:, :]))
        c_v.after(V.tensor_copy(tile_f[:, :], tile_i[:, :]))
        c_v.after(V.tensor_copy(place[:, 0:1], place_i[:, :]))
        c_v.after(V.tensor_scalar(out=place[:, 1:2], in0=place_i[:, :], scalar1=-1.0, scalar2=None, op0=ALU.mult))
        c_v.after(V.memset(ones[:, :], 1.0))
        k_const = c_v.after(V.memset(eps[:, :], EPS))
        wait(V, k_const)

        def step_tables():
            df = flat_ring[0:EP, 3 * D:4 * D]
            junk = flat_ring[0:EP, 4 * D:5 * D]
            cnt = sb("cnt", [EP, TILES - 1])
            wait(V, k_ed)
            m = c_v.after(V.tensor_copy(df.rearrange("p (c e) -> p c e", c=EC), ed[:, :, 1, :]))
            wait(V, m)
            for t in range(1, TILES):
                m = c_v.after(V.tensor_scalar(out=junk, in0=df, scalar1=float(t * TN), scalar2=None, op0=ALU.is_lt,
                                              op1=ALU.add, accum_out=cnt[:, t - 1:t]))
                wait(V, m)
                if t % 2 == 0:
                    yield
            wait(P, m)
            m = c_p.after(P.matmul(bank[0][:, 0:TILES - 1], ones[0:EP, :], cnt[:, :], start=True, stop=True))
            thr = sb("thr", [128, TILES - 1])
            lim = sb("lim", [RS, RB])
            tstep = sb("tstep", [RS, RB])
            tn_step = sb("tn_step", [RS, RB])
            gstep = sb("gstep", [RS, RB], I32)
            thr_junk = sb("thr_junk", [RS, TILES - 1])
            wait(V, m)
            c_v.after(V.tensor_tensor(thr[:, :], bank[0][:, 0:TILES - 1], tile_f[:, :], ALU.add))
            m = c_v.after(V.tensor_scalar(out=lim[:, :], in0=step_f[:, :], scalar1=1.0, scalar2=float(CE),
                                          op0=ALU.add, op1=ALU.mult))
            wait(V, m)
            for b in range(RB):
                m = c_v.after(V.tensor_scalar(out=thr_junk[:, :], in0=thr[0:RS, :], scalar1=lim[:, b:b + 1], scalar2=None,
                                              op0=ALU.is_lt, op1=ALU.add, accum_out=tstep[:, b:b + 1]))
                wait(V, m)
            c_v.after(V.tensor_scalar(out=tn_step[:, :], in0=tstep[:, :], scalar1=float(TN), scalar2=None, op0=ALU.mult))
            k_g = c_v.after(V.tensor_tensor(gstep[:, :], step_f[:, :], tstep[:, :], ALU.subtract))
            rows = [flat_ring[0:RS, (3 + b) * D:(3 + b) * D + 3 * CE] for b in range(RB)]
            wait(G, k_g, k_er)
            for b in range(RB):
                k_pt = c_pt.after(G.indirect_dma_start(
                    out=rows[b].bitcast(I32), out_offset=None, in_=edge_rows[:, :],
                    in_offset=bass.IndirectOffsetOnAxis(ap=gstep[:, b:b + 1], axis=0)), 16)
            yield
            yield
            wait(V, k_pt, k_g)
            rsf = big[0:RS, 0:RB * 2 * CE].rearrange("p (b a e) -> p b a e", b=RB, a=2)
            for b in range(RB):
                ri = rows[b].bitcast(I32)
                c_v.after(V.tensor_copy(rsf[:, b, 0, :], ri[:, 0:CE]))
                c_v.after(V.tensor_scalar(out=rsf[:, b, 1, :], in0=ri[:, CE:2 * CE], scalar1=tn_step[:, b:b + 1],
                                          scalar2=None, op0=ALU.subtract))
                m = c_v.after(V.tensor_copy(dstf[:, b, :], ri[:, CE:2 * CE]))
            wait(V, m)
            dst_rows = big[0:RS, RB * 2 * CE:RB * 2 * CE + RB * CE // 2].bitcast(BF16).rearrange("p (b e) -> p b e", b=RB)
            mp = c_v.after(V.tensor_copy(dst_rows, rsf[:, :, 1, :]))
            wait(S, mp)
            marks["dst_places"] = c_dpl.after(S.dma_start(dst_places.rearrange("(b p) e -> p b e", p=RS), dst_rows), 16)
            wait(P, m, k_ident, k_pt)
            tb = [0, 1, 2, 3]
            for b in range(RB):
                for a in range(3):
                    piece = rows[b][:, 2 * CE:3 * CE] if a == 2 else rsf[:, b, a, :]
                    m = c_p.after(P.transpose(bank[tb[a]][:, b * RS:(b + 1) * RS], piece, ident[0:RS, 0:RS]))
                m = c_p.after(P.transpose(bank[tb[3]][0:1, b * RS:(b + 1) * RS], tstep[:, b:b + 1], ident[0:RS, 0:RS]))
            yield
            wait(V, m)
            c_v.after(V.tensor_copy(src_t[:, :], bank[tb[0]][:, 0:STEPS]))
            c_v.after(V.tensor_copy(dl_t[:, :], bank[tb[1]][:, 0:STEPS]))
            c_v.after(V.tensor_copy(w_t[:, :], bank[tb[2]][:, 0:STEPS]))
            marks["tables"] = c_v.after(V.tensor_copy(tile_row[:, :], bank[tb[3]][0:1, 0:STEPS]))
            wait(V, marks["tables"])
            m = c_v.after(V.tensor_scalar(out=masked[:, :, :], in0=rsf[:, :, 1, :], scalar1=0.0, scalar2=None, op0=ALU.is_ge))
            wait(V, m)
            m = c_v.after(V.scalar_tensor_tensor(out=masked[:, :, :], in0=rsf[:, :, 1, :], scalar=float(TN),
                                                 in1=masked[:, :, :], op0=ALU.is_lt, op1=ALU.mult))
            wait(V, m)
            m = marks["masked"] = c_v.after(V.tensor_scalar(out=masked[:, :, :], in0=masked[:, :, :], scalar1=-1.0,
                                                            scalar2=BIG, op0=ALU.add, op1=ALU.mult))
            wait(V, m)

        def degrees():
            hot = big[:, 0:TILES * STEPS // 2].bitcast(BF16).rearrange("p (t i) -> p t i", t=TILES)
            hi, lo, srcm = (stage[:, n * STEPS:(n + 1) * STEPS] for n in range(3))
            lo_hot = stage[:, 3 * STEPS:3 * STEPS + 4 * 64].bitcast(BF16).rearrange("p (q n) -> p q n", q=4)
            lo_abs = stage[:, 3 * STEPS + 4 * 64:3 * STEPS + 8 * 64].bitcast(BF16).rearrange("p (q n) -> p q n", q=4)
            m = c_v.after(V.tensor_scalar(out=srcm, in0=dl_t[:, :], scalar1=0.0, scalar2=None, op0=ALU.is_ge))
            wait(V, m)
            m = c_v.after(V.scalar_tensor_tensor(out=srcm, in0=dl_t[:, :], scalar=float(TN), in1=srcm, op0=ALU.is_lt, op1=ALU.mult))
            wait(V, m)
            m = c_v.after(V.tensor_scalar(out=srcm, in0=srcm, scalar1=-1.0, scalar2=-float(N), op0=ALU.add, op1=ALU.mult))
            yield
            wait(V, m)
            m = c_v.after(V.tensor_tensor(srcm, srcm, src_t[:, :], ALU.add))
            yield
            wait(V, m)
            m = c_v.after(V.tensor_scalar(out=hi, in0=srcm, scalar1=float(TN), scalar2=None, op0=ALU.is_ge))
            for t in range(2, TILES + 1):
                yield
                wait(V, m)
                m = c_v.after(V.scalar_tensor_tensor(out=hi, in0=srcm, scalar=float(t * TN), in1=hi, op0=ALU.is_ge, op1=ALU.add))
            yield
            wait(V, m)
            m = k_lo = c_v.after(V.scalar_tensor_tensor(out=lo, in0=hi, scalar=float(TN), in1=srcm, op0=ALU.mult, op1=ALU.subtract))
            c_v.after(V.tensor_copy(src_tile[:, :], hi[:, STEPS - US:STEPS]))
            wait(P, k_lo)
            for k in range(2):
                last = P.transpose(bank[5][0:US // 2, k * CE:(k + 1) * CE], lo[:, STEPS - US + k * US // 2:STEPS - US + (k + 1) * US // 2],
                                   ident[:, :])
            m = c_p.after(last)
            wait(V, m)
            src_rows = stage[0:US // 2, 3 * STEPS + 8 * 64:3 * STEPS + 8 * 64 + CE].bitcast(BF16)
            m = c_v.after(V.tensor_copy(src_rows, bank[5][0:US // 2, 0:2 * CE]))
            wait(S, m)
            marks["src_places"] = c_spl.after(S.dma_start(src_places.rearrange("(k p) e -> p k e", k=2),
                                                         src_rows.rearrange("p (k e) -> p k e", k=2)), 16)
            wait(V, marks["dst_places"])
            for t in range(TILES):
                yield
                m = c_v.after(V.tensor_scalar(out=hot[:, t, :], in0=hi, scalar1=float(t), scalar2=None, op0=ALU.is_equal))
            wait(A, m, k_lo)
            wait(P, m)
            used = {}
            for i in range(STEPS):
                q = i % 4
                m = c_a.after(A.activation(lo_abs[:, q, 0:TN], node_iota[:, :], ACT.Abs, bias=lo[:, i:i + 1]))
                wait(A, m, used.get(i - 4))
                m = c_a.after(A.activation(lo_hot[:, q, 0:TN], lo_abs[:, q, 0:TN], ACT.Relu, bias=ones[:, 0:1], scale=-1.0))
                wait(P, m)
                used[i] = c_p.after(P.matmul(bank[4][0:TN, 0:TILES], lo_hot[:, q, 0:TN], hot[:, :, i],
                                             start=(i == 0), stop=(i == STEPS - 1)))
                if i % 3:
                    yield
            wait(V, used[STEPS - 1])
            m = c_v.after(V.tensor_scalar(out=dis[:, :], in0=bank[4][0:TN, 0:TILES], scalar1=1.0, scalar2=None, op0=ALU.add))
            free["bankT", 0] = m
            wait(A, m)
            m = c_a.after(A.activation(dis[:, :], dis[:, :], ACT.Sqrt))
            wait(V, m)
            marks["dis"] = c_v.after(V.reciprocal(dis[:, :], dis[:, :]))
            wait(A, marks["dis"])

        free = {}
        marks = {}

        def split(high, low, value, ready):
            wait(A, ready)
            m = c_a.after(A.copy(high, value))
            wait(V, ready, m)
            m2 = c_v.after(V.tensor_tensor(low, value, high.bitcast(F32), ALU.subtract))
            return m2

        def split_weight(high, low, raw, ready):
            for k in range(KB):
                m = split(high[:, k, :], low[:, k, :], raw[:, k, :], ready)
            return m

        def norm_stats(t, *before, then_std=True):
            q = t % 4
            wait(V, *before)
            m = c_v.after(V.bn_stats(stats[:, q, :], x[0:TN, t, :]))
            wait(V, m, free.get(("mv", q)))
            marks["mv", t] = c_v.after(V.bn_aggr(mv[:, q, :], stats[:, q, :]))
            if then_std:
                norm_std(t)

        def norm_std(t):
            q = t % 4
            wait(A, marks["mv", t])
            marks["std", t] = c_a.after(A.activation(rstd[:, q, 0:1], mv[:, q, 1:2], ACT.Sqrt, bias=eps[0:TN, :]))

        def norm_relu(t, dest, dest_free=None):
            q = t % 4
            wait(V, marks["std", t])
            m = c_v.after(V.reciprocal(rstd[:, q, 0:1], rstd[:, q, 0:1]))
            wait(V, m)
            m = c_v.after(V.tensor_scalar(out=rstd[:, q, 1:2], in0=mv[:, q, 0:1], scalar1=-1.0,
                                          scalar2=rstd[:, q, 0:1], op0=ALU.mult, op1=ALU.mult))
            wait(A, m, dest_free)
            free["mv", q] = c_a.after(A.activation(dest, x[0:TN, t, :], ACT.Relu, bias=rstd[:, q, 1:2], scale=rstd[:, q, 0:1]))
            return free["mv", q]

        def transpose_rows(key, t, rows_ap, ready):
            q = t % 2
            wait(P, ready, free.get(("bankT", q)))
            for k in range(KB):
                last = P.transpose(bank[4 + q][:, k * TN:(k + 1) * TN], rows_ap[:, k * 128:(k + 1) * 128], ident[0:TN, 0:TN])
            marks[key, t] = c_p.after(last)

        def high_half(key, t, ready, relu=False):
            q = t % 2
            wait(A, ready, free.get(("hT", q)))
            marks[key, t] = c_a.after(A.activation(hTh[:, q, :, :].rearrange("p k n -> p (k n)"), bank[4 + q][:, 0:KB * TN],
                                                   ACT.Relu if relu else ACT.Copy))

        def low_half(key, t, ready, relu=False):
            q = t % 2
            b = bank[4 + q][:, 0:KB * TN]
            high = hTh[:, q, :, :].rearrange("p k n -> p (k n)").bitcast(F32)
            low = hTl[:, q, :, :].rearrange("p k n -> p (k n)")
            wait(V, ready)
            if relu:
                ins = V.scalar_tensor_tensor(out=low, in0=b, scalar=0.0, in1=high, op0=ALU.max, op1=ALU.subtract)
            else:
                ins = V.tensor_tensor(low, b, high, ALU.subtract)
            free["bankT", q] = marks[key, t] = c_v.after(ins)

        def product(out_ap, q, high, low):
            last = None
            for k in range(KB):
                for n, (a, b) in enumerate(((hTh, high), (hTh, low), (hTl, high))):
                    last = P.matmul(out_ap, a[:, q, k, :], b[:, k, :], start=(k == 0 and n == 0),
                                    stop=(k == KB - 1 and n == 2))
            return last

        def project(t, ready, high, low):
            q = t % 2
            wait(P, ready, free.get(("bankZ", q)))
            free["hT", q] = c_p.after(product(bank[6 + q][0:TN, :], q, high, low))
            return free["hT", q]

        def store(t, dest, rows_ap, ready):
            wait(S, ready)
            return c_st[t % 3].after(S.dma_start(dest[t * TN:(t + 1) * TN, :], rows_ap), 16)

        LOADED = 8
        tile_regs = {}

        def step_tile(engine, name, i):
            if (name, 0) not in tile_regs:
                for n in range(LOADED):
                    tile_regs[name, n] = engine.alloc_register(f"tile_{name}{n}")
            if i % LOADED == 0:
                engine.reg_load([tile_regs[name, n] for n in range(LOADED)], tile_row[0:1, i:i + LOADED])
            return nc.s_assert_within(engine.snap(tile_regs[name, i % LOADED]), 0, TILES - 1,
                                      skip_runtime_bounds_check_because="a count of TILES - 1 comparisons")

        done = {"pe": [], "acc": None}

        def aggregate(layer, target, weights, table_ready, target_ready, alpha=None, beside=None, also=None):
            base = len(done["pe"])
            sels, gathered, scaled, acc_marks = {}, {}, {}, {}
            wait(V, *target_ready)
            wait(G, *table_ready)

            def select(i):
                n = base + i
                if not weights:
                    if i % SB == 0:
                        wait(V, done["pe"][n + SB - 1 - SELS])
                        ins = V.tensor_tensor(sel[:, n % SELS:n % SELS + SB, :], node_iota[:, None, :].to_broadcast([CE, SB, TN]),
                                              dl_t[:, i:i + SB, None].to_broadcast([CE, SB, TN]), ALU.is_equal)
                        sels[i // SB] = c_v.after(ins)
                    return
                if n >= SELS:
                    wait(V, done["pe"][n - SELS])
                ins = V.tensor_scalar(out=sel[:, n % SELS, :], in0=node_iota[:, :], scalar1=dl_t[:, i:i + 1],
                                      scalar2=w_t[:, i:i + 1], op0=ALU.is_equal, op1=ALU.mult)
                sels[i] = c_v.after(ins)

            def gather(i):
                n = base + i
                if n >= RING:
                    wait(G, done["pe"][n - RING])
                gathered[i] = c_ring[n % RING].after(G.indirect_dma_start(
                    out=ring[:, n % RING, :], out_offset=None, in_=table[layer][:, :],
                    in_offset=bass.IndirectOffsetOnAxis(ap=src_t[:, i:i + 1], axis=0)), 16)

            def scale(i):
                slot = ring[:, (base + i) % RING, :].rearrange("p (h j) -> p h j", h=H)
                HV = H // 2 - (i % 4 == 0)
                wait(V, gathered[i])
                dve_part = c_v.after(V.tensor_tensor(slot[:, 0:HV, :], slot[:, 0:HV, :],
                                                     alpha[:, i, 0:HV, None].to_broadcast([CE, HV, DP]), ALU.mult))
                wait(A, gathered[i])
                for h in range(HV, H):
                    last = A.activation(slot[:, h, :], slot[:, h, :], ACT.Copy, scale=alpha[:, i, h:h + 1])
                scaled[i] = (dve_part, c_a.after(last))

            for i in range(STEPS + AHEAD):
                j = i - AHEAD
                if i < STEPS:
                    gather(i)
                    select(i)
                if alpha is not None and 0 <= i - SCALE_AHEAD < STEPS:
                    scale(i - SCALE_AHEAD)
                if j < 0:
                    continue
                n = base + j
                wait(P, *(scaled[j] if alpha is not None else (gathered[j],)))
                wait(P, sels[j if weights else j // SB], acc_marks.get(j - NAGG))
                last = P.matmul(bank[n % NAGG][0:TN, :], sel[:, n % SELS, :], ring[:, n % RING, :], start=True, stop=True)
                if also is not None:
                    last = also(j, sel[:, n % SELS, :])
                mark = c_p.after(last)
                done["pe"].append(mark)
                t = step_tile(V, "v", j)
                wait(V, mark, done["acc"])
                part = target[0:TN, bass.ds(t, 1), :].rearrange("p a d -> p (a d)")
                done["acc"] = acc_marks[j] = c_v.after(V.tensor_tensor(part, part, bank[n % NAGG][0:TN, :], ALU.add))
                if beside is not None:
                    next(beside, None)
            if beside is not None:
                for _ in beside:
                    pass
            return done["acc"]

        def pipeline(stages, beside=None):
            for n in range(TILES + max(lag for lag, _ in stages)):
                for lag, stage_of in stages:
                    if 0 <= n - lag < TILES:
                        stage_of(n - lag)
                if beside is not None:
                    next(beside, None)
            if beside is not None:
                for _ in beside:
                    pass

        def last_stores(key):
            return [marks[key, t] for t in range(TILES - 3, TILES)]

        k_w0 = split_weight(wh, wl, flat_ring[:, 7 * D:11 * D].rearrange("p (k d) -> p k d", k=KB), k_w)
        wait(P, k_w0, k_ident)
        wait(A, k_const)

        def l0_stats(t):
            norm_stats(t, k_x[t // XQ])

        def l0_relu(t):
            wait(A, k_x[t // XQ])
            marks["h", t] = norm_relu(t, hbuf(t % 2), marks.get(("tr", t - 2)))

        def plain_tr(t):
            transpose_rows("tr", t, hbuf(t % 2), marks["h", t])

        def plain_high(t):
            high_half("hTh", t, marks["tr", t])

        def plain_low(t):
            low_half("hT", t, marks["hTh", t])

        def l0_mm(t):
            marks["z", t] = project(t, marks["hT", t], wh, wl)

        def l0_out(t):
            wait(A, marks["z", t], marks.get(("st", t - 3)))
            free["bankZ", t % 2] = m = c_a.after(A.copy(zbuf(t % 3), bank[6 + t % 2][0:TN, :]))
            marks["st", t] = store(t, table[0], zbuf(t % 3), m)
            wait(G, marks["hT", t])
            marks["zero", t] = c_g.after(G.memset(acc[0:TN, t, :], 0.0))

        pipeline([(3, plain_high), (1, l0_relu), (0, l0_stats), (5, l0_out), (3, plain_low), (4, l0_mm), (2, plain_tr)],
                 beside=step_tables())

        def beside_l0():
            yield from degrees()
            wait(S, marks["dis"], marks["src_places"])
            m = c_w.after(S.dma_start(raw_w, W1_in.rearrange("(k p) d -> p k d", p=128)), 16)
            k_b = c_w.after(S.dma_start(bias_bc[:, :], b1_in.rearrange("(a d) -> a d", a=1).to_broadcast([TN, D])), 16)
            for _ in range(8):
                yield
            wait(P, k_b)
            wait(V, k_b)
            for k in range(KB):
                wait(P, marks.get(("wsplit", k - 2)))
                for j in range(KB):
                    last = P.transpose(bank[5 + k % 2][:, j * 128:(j + 1) * 128], raw_w[:, j, k * 128:(k + 1) * 128], ident[:, :])
                m = marks["wread"] = c_p.after(last)
                yield
                marks["wsplit", k] = split(wh[:, k, :], wl[:, k, :], bank[5 + k % 2][:, :], m)
            wait(P, m, marks["wsplit", KB - 1])
            wait(A, marks["wread"])

        wait(V, marks["tables"], marks["zero", TILES - 1])
        wait(G, marks["tables"])
        wait(A, marks["masked"], *last_stores("st"))
        k_acc = aggregate(0, acc, True, last_stores("st"), last_stores("st"), beside=beside_l0())

        def l1_stats(t):
            m = c_v.after(V.scalar_tensor_tensor(out=x[0:TN, t, :], in0=acc[0:TN, t, :], scalar=0.0, in1=x[0:TN, t, :],
                                                 op0=ALU.max, op1=ALU.add))
            marks["xr", t] = m
            norm_stats(t, m)

        def l1_relu(t):
            wait(A, marks["xr", t])
            marks["h", t] = norm_relu(t, hbuf(t % 2), marks["tr", (t - 2) % TILES])

        def l1_out(t):
            wait(V, marks["z", t], marks.get(("scaled", t - 3)))
            free["bankZ", t % 2] = m = c_v.after(V.tensor_tensor(zbuf(t % 3), bank[6 + t % 2][0:TN, :], bias_bc[:, :], ALU.add))
            wait(A, m)
            marks["scaled", t] = m = c_a.after(A.activation(acc[0:TN, t, :], zbuf(t % 3), ACT.Copy, scale=dis[:, t:t + 1]))
            marks["st", t] = store(t, table[1], acc[0:TN, t, :], m)

        wait(V, k_acc)
        pipeline([(3, plain_high), (1, l1_relu), (0, l1_stats), (5, l1_out), (3, plain_low), (4, l0_mm), (2, plain_tr)])
        b2_bc = stage[0:TN, 4 * D:5 * D]

        def beside_l1():
            wait(S, marks["scaled", TILES - 1], marks["hT", TILES - 1], marks["z", TILES - 1])
            m = c_w.after(S.dma_start(raw_w, G1_in.rearrange("(k p) d -> p k d", p=128)), 16)
            for _ in range(12):
                yield
            for k in range(KB):
                marks["g1w"] = split(wh[:, k, :], wl[:, k, :], raw_w[:, k, :], m)
                yield
            wait(S, marks["g1w"])
            c_w2.after(S.dma_start(bias_bc[:, :], g1_in.rearrange("(a d) -> a d", a=1).to_broadcast([TN, D])), 16)
            marks["biases"] = c_w2.after(S.dma_start(b2_bc, g2_in.rearrange("(a d) -> a d", a=1).to_broadcast([TN, D])), 16)
            wait(A, marks["g1w"])
            wait(V, marks["biases"])

        k_acc = aggregate(1, acc, False, last_stores("st"), last_stores("st"), beside=beside_l1())

        wait(A, k_acc)

        def l2_sum(t):
            wait(A, marks.get(("xadd", t - 2)))
            marks["r2", t] = c_a.after(A.activation(hbuf(t % 2), acc[0:TN, t, :], ACT.Relu, scale=dis[:, t:t + 1]))

        def l2_stats(t):
            wait(V, marks["r2", t])
            marks["xadd", t] = c_v.after(V.tensor_tensor(x[0:TN, t, :], x[0:TN, t, :], hbuf(t % 2), ALU.add))
            norm_stats(t, marks["xadd", t], then_std=False)

        def l2_relu(t):
            wait(A, marks["xadd", t])
            m = marks["h2", t] = norm_relu(t, acc[0:TN, t, :])
            marks["st", t] = store(t, table[2], acc[0:TN, t, :], m)

        pipeline([(2, norm_std), (0, l2_sum), (3, l2_relu), (1, l2_stats)])

        FW = RB * CE
        keep, nlast, pf, pb_ = (big[0:RS, n * FW:(n + 1) * FW].rearrange("p (b e) -> p b e", b=RB) for n in range(4))
        row8 = stage[0:H, 0:4 * (STEPS + 2)].rearrange("p (a i) -> p a i", a=4)
        r8x = stage[0:H, 4 * (STEPS + 2):4 * (STEPS + 2) + STEPS]
        zero = sb("zero", [RS, CE])

        def to_row8(lane_of_edge8, row, shift, b, bk, ready, free_mark):
            wait(P, ready, free_mark)
            m = c_p.after(P.transpose(bank[bk][0:H, 0:RS], edge8[:, b, lane_of_edge8, :], ident[0:RS, 0:RS]))
            wait(V, m)
            return c_v.after(V.tensor_copy(row8[:, row, shift + b * RS:shift + (b + 1) * RS], bank[bk][0:H, 0:RS]))

        def to_back8(row_ap, lane, b, bk, ready, free_mark):
            wait(P, ready, free_mark)
            m = c_p.after(P.transpose(bank[bk][0:RS, 0:H], row_ap, ident[0:H, 0:H]))
            wait(V, m)
            return c_v.after(V.tensor_copy(back8[:, b, lane, :], bank[bk][0:RS, 0:H]))

        def beside_l2():
            for t in range(TILES):
                m = c_v.after(V.tensor_tensor(x[0:TN, t, :], x[0:TN, t, :], b2_bc, ALU.add))
                yield
                yield
                yield
            c_v.after(V.tensor_tensor(keep[:, :, 1:CE], dstf[:, :, 1:CE], dstf[:, :, 0:CE - 1], ALU.is_equal))
            c_v.after(V.tensor_copy(edge8[:, :, 0, :], dstf[:, :, 0:1].to_broadcast([RS, RB, H])))
            c_v.after(V.tensor_copy(edge8[:, :, 1, :], dstf[:, :, CE - 1:CE].to_broadcast([RS, RB, H])))
            c_v.after(V.memset(zero[:, :], 0.0))
            wait(V, m)
            m = c_v.after(V.memset(row8, -1.0))
            wait(V, m)
            last = None
            for b in range(RB):
                for s in range(2):
                    last = to_row8(s, s, 1 + s, b, 4, m, last)
                    yield
            wait(V, last)
            m = c_v.after(V.memset(row8[:, 2, :], 0.0))
            wait(V, m)
            m = last = c_v.after(V.tensor_tensor(row8[:, 2, 1:STEPS + 1], row8[:, 0, 1:STEPS + 1], row8[:, 1, 1:STEPS + 1],
                                                 ALU.is_equal))
            for b in range(RB):
                for lane in range(2):
                    last = to_back8(row8[:, 2, 1 + lane + b * RS:1 + lane + (b + 1) * RS], lane, b, 4, m, last)
                    yield
            wait(V, last)
            c_v.after(V.tensor_copy(keep[:, :, 0:1], back8[:, :, 0, 0:1]))
            m = c_v.after(V.tensor_copy(nlast[:, :, CE - 1:CE], back8[:, :, 1, 0:1]))
            wait(V, m)
            m = c_v.after(V.tensor_copy(nlast[:, :, 0:CE - 1], keep[:, :, 1:CE]))
            wait(V, m)
            for b in range(RB):
                c_v.after(V.tensor_tensor_scan(pf[:, b, :], keep[:, b, :], zero[:, :], 1.0, ALU.mult, ALU.add))
                yield
                m = c_v.after(V.tensor_tensor_scan(pb_[:, b, ::-1], nlast[:, b, ::-1], zero[:, :], 1.0, ALU.mult, ALU.add))
                yield
            wait(V, m)
            c_v.after(V.tensor_copy(edge8[:, :, 0, :], pf[:, :, CE - 1:CE].to_broadcast([RS, RB, H])))
            m = c_v.after(V.tensor_copy(edge8[:, :, 1, :], pb_[:, :, 0:1].to_broadcast([RS, RB, H])))
            last = None
            for b in range(RB):
                for s in range(2):
                    last = to_row8(s, 2 + s, 1, b, 4, m, last)
                    yield
            free["bankT", 0] = last
            wait(V, last)
            marks["flags"] = c_v.after(V.tensor_copy(flags8[:, :, :], row8[:, 2:4, 1:STEPS + 1]))
            wait(V, marks["flags"])
            wait(A, marks["flags"])

        flags8 = sb("flags8", [H, 2, STEPS])
        k_acc = aggregate(2, acc, False, last_stores("st"), last_stores("st"), beside=beside_l2())

        raw2 = flat_ring[:, 0:KB * D].rearrange("p (k d) -> p k d", k=KB)
        raw3 = flat_ring[:, KB * D:2 * KB * D].rearrange("p (k d) -> p k d", k=KB)
        raw3h = flat_ring[:, KB * D:2 * KB * D].rearrange("p (k h j) -> p k h j", k=KB, h=H)
        aw_bc = flat_ring[:, 2 * KB * D:(2 * KB + 2) * D].rearrange("p (s h j) -> p s h j", s=2, h=H)
        wb_bc = flat_ring[0:TN, (2 * KB + 2) * D:(2 * KB + 3) * D]
        wait(S, done["pe"][-1])
        k_w2 = c_w2.after(S.dma_start(raw2, G2_in.rearrange("(k p) d -> p k d", p=128)), 16)
        for k in range(KB):
            c_w.after(S.dma_start(raw3h[:, k, :, :], Ws_in[:, k * 128:(k + 1) * 128, :].rearrange("h p j -> p h j")), 16)
        for s in range(2):
            c_w.after(S.dma_start(aw_bc[:, s, :, :], aw_in[:, s * DP:(s + 1) * DP].rearrange("(a h) j -> a h j", a=1)
                                  .to_broadcast([128, H, DP])), 16)
        c_w.after(S.dma_start(wb_bc, Wb_in.rearrange("(a h) j -> a (h j)", a=1).to_broadcast([TN, D])), 16)
        k_w3 = c_w.after(S.dma_start(ab_bc[:, :], ab_in.rearrange("(a h) -> a h", a=1).to_broadcast([TN, H])), 16)

        def score_weights():
            prod = flat_ring[:, (2 * KB + 3) * D:(2 * KB + 4) * D].rearrange("p (h j) -> p h j", h=H)
            yield
            yield
            yield
            wait(V, k_w3)
            m = None
            for s in range(2):
                for k in range(KB + 1):
                    wait(V, m)
                    if k < KB:
                        m = c_v.after(V.tensor_tensor(prod, raw3h[:, k, :, :], aw_bc[:, s, :, :], ALU.mult))
                        wait(V, m)
                        m = c_v.after(V.tensor_reduce(wa[:, k, s * H:(s + 1) * H], prod, axis=AX.X, op=ALU.add))
                    else:
                        m = c_v.after(V.tensor_tensor(prod[0:TN], wb_bc.rearrange("p (h j) -> p h j", h=H), aw_bc[0:TN, s, :, :], ALU.mult))
                        wait(V, m)
                        m = c_v.after(V.tensor_reduce(sc_bias[:, s * H:(s + 1) * H], prod[0:TN], axis=AX.X, op=ALU.add))
                    yield
            wait(V, m)
            m = c_v.after(V.tensor_tensor(sc_bias[:, 0:H], sc_bias[:, 0:H], ab_bc[:, :], ALU.add))
            marks["wa"] = m

        wait(P, k_acc)
        free["hT", 0] = free["hT", 1] = None

        def g_tr(t):
            transpose_rows("gtr", t, acc[0:TN, t, :], None)

        def g_high(t):
            high_half("g1h", t, marks["gtr", t])

        def g_low(t):
            low_half("g1T", t, marks["g1h", t])

        def g_mm1(t):
            marks["g1", t] = project(t, marks["g1T", t], wh, wl)

        def g_bias(t):
            wait(V, marks["g1", t], marks["gtr", t])
            free["bankZ", t % 2] = marks["z1", t] = c_v.after(V.tensor_tensor(
                acc[0:TN, t, :], bank[6 + t % 2][0:TN, :], bias_bc[:, :], ALU.add))

        pipeline([(1, g_high), (3, g_bias), (1, g_low), (2, g_mm1), (0, g_tr)], beside=score_weights())

        wait(A, marks["g1", TILES - 1])
        wait(V, marks["g1", TILES - 1])
        k_w2_split = split_weight(wh, wl, raw2, k_w2)

        def rows_T(t):
            return acc[:, t, 0:KB * TN].rearrange("p (k n) -> p k n", k=KB)

        wait(A, marks["wa"])

        def g_tr2(t):
            transpose_rows("gtr2", t, acc[0:TN, t, :], marks["z1", t])

        def g_high2(t):
            high_half("g2h", t, marks["gtr2", t], relu=True)

        def g_low2(t):
            low_half("g2T", t, marks["g2h", t], relu=True)

        def g_mm2(t):
            wait(P, k_w2_split)
            marks["g2", t] = project(t, marks["g2T", t], wh, wl)

        def g_add(t):
            wait(V, marks["g2", t])
            free["bankZ", t % 2] = marks["x", t] = c_v.after(V.tensor_tensor(x[0:TN, t, :], x[0:TN, t, :],
                                                                             bank[6 + t % 2][0:TN, :], ALU.add))
            norm_stats(t, marks["x", t], then_std=False)

        def l3_relu(t):
            wait(A, marks["x", t])
            marks["h", t] = norm_relu(t, acc[0:TN, t, :], marks["gtr2", t])

        def s_tr(t):
            wait(P, marks["h", t], marks.get(("rows_T", t - 2)))
            for k in range(KB):
                last = P.transpose(bank[2 + t % 2][:, k * TN:(k + 1) * TN], acc[0:TN, t, k * 128:(k + 1) * 128], ident[0:TN, 0:TN])
            marks["str", t] = c_p.after(last)

        def s_copy(t):
            wait(A, marks["str", t])
            marks["rows_T", t] = c_a.after(A.copy(acc[:, t, 0:KB * TN], bank[2 + t % 2][:, 0:KB * TN]))

        def s_mm(t):
            wait(P, marks["wa"], marks["rows_T", t], marks.get(("sc", t - 2)))
            for k in range(KB):
                last = P.matmul(bank[t % 2][0:TN, 0:2 * H], rows_T(t)[:, k, :], wa[:, k, :], start=(k == 0), stop=(k == KB - 1))
            marks["s", t] = c_p.after(last)

        def s_out(t):
            q = t % 2
            wait(V, marks["s", t])
            c_v.after(V.tensor_tensor(t_all[:, t, :], bank[q][0:TN, 0:H], sc_bias[:, 0:H], ALU.add))
            m = marks["sc", t] = c_v.after(V.tensor_tensor(u_all[:, t, :], bank[q][0:TN, H:2 * H], sc_bias[:, H:2 * H], ALU.add))
            wait(S, m)
            marks["us", t] = c_us[q].after(S.dma_start(score_table[t * TN:(t + 1) * TN, :], u_all[:, t, :]), 16)

        pipeline([(1, g_high2), (4, norm_std), (7, s_copy), (5, l3_relu), (3, g_add), (1, g_low2), (9, s_out),
                  (2, g_mm2), (0, g_tr2), (6, s_tr), (8, s_mm)])
        stored_u = [marks["us", t] for t in range(TILES - 2, TILES)]

        wait(A, marks["g2", TILES - 1])
        wait(V, marks["g2", TILES - 1])
        k_w = split_weight(wh, wl, raw3, k_w3)
        wait(P, k_w)

        def l3_high(t):
            q = t % 2
            wait(A, marks["rows_T", t], free.get(("hT", q)))
            marks["h3h", t] = c_a.after(A.copy(hTh[:, q, :, :].rearrange("p k n -> p (k n)"), acc[:, t, 0:KB * TN]))

        def l3_low(t):
            q = t % 2
            wait(V, marks["h3h", t])
            marks["h3T", t] = c_v.after(V.tensor_tensor(hTl[:, q, :, :].rearrange("p k n -> p (k n)"), acc[:, t, 0:KB * TN],
                                                        hTh[:, q, :, :].rearrange("p k n -> p (k n)").bitcast(F32), ALU.subtract))

        def l3_mm(t):
            marks["z3", t] = project(t, marks["h3T", t], wh, wl)

        def l3_out(t):
            wait(V, marks["z3", t], marks.get(("st3", t - 3)))
            m = free["bankZ", t % 2] = c_v.after(V.tensor_tensor(zbuf(t % 3), bank[6 + t % 2][0:TN, :], wb_bc, ALU.add))
            marks["st3", t] = store(t, table[3], zbuf(t % 3), m)

        TH = TILES * H
        t3 = stage[0:TN, 0:3 * TH // 2].bitcast(BF16).rearrange("p (t s h) -> p t s h", s=3, h=H)
        u3 = stage[0:TN, 3 * TH // 2:3 * TH].bitcast(BF16).rearrange("p (s t h) -> p s t h", s=3, h=H)
        rem = [stage[0:TN, (3 + n) * TH:(4 + n) * TH].rearrange("p (t h) -> p t h", h=H) for n in range(2)]
        m = marks["sc", TILES - 1]
        for n in range(3):
            wait(V, m)
            rests = (t_all[:, :, :], u_all[:, :, :]) if n == 0 else rem
            parts = (t3[:, :, n, :], u3[:, n, :, :])
            for part, rest in zip(parts, rests):
                m = c_v.after(V.tensor_copy(part, rest))
            wait(V, m)
            if n < 2:
                for part, rest, left in zip(parts, rests, rem):
                    m = c_v.after(V.tensor_tensor(left, rest, part, ALU.subtract))
        parts_ready = m
        pipeline([(0, l3_high), (2, l3_out), (0, l3_low), (1, l3_mm)])
        stored = last_stores("st3")

        ue = big[:, 4 * FW:4 * FW + STEPS * H].rearrange("p (i h) -> p i h", h=H)
        te = flat_ring[:, 0:STEPS * H].rearrange("p (i h) -> p i h", h=H)
        backwards = flat_ring[0:RS, STEPS * H:STEPS * H + H // 2 * CE]
        cont, cont_back = (flat_ring[0:RS, (8 + n) * FW:(9 + n) * FW].rearrange("p (b e) -> p b e", b=RB) for n in range(2))
        ex = flat_ring[0:RS, 0:RB * H * CE].rearrange("p (b h e) -> p b h e", b=RB, h=H)
        flat_acc = acc[:, :, :].rearrange("p a b -> p (a b)")
        WR = RB * H * CE
        zr, fr = (flat_acc[0:RS, n * WR:(n + 1) * WR].rearrange("p (b h e) -> p b h e", b=RB, h=H) for n in range(2))
        GW = UG * CE
        dp, sp, dp_hot, sp_hot = ([flat_acc[0:TN, 2 * WR + (2 * n + q) * GW // 2:2 * WR + (2 * n + q + 1) * GW // 2].bitcast(BF16)
                                   for q in range(2)] for n in range(4))
        dp_hot.append(flat_acc[0:TN, 3 * WR:3 * WR + GW // 2].bitcast(BF16))
        sp_hot.append(stage[0:TN, 9 * TILES * H:9 * TILES * H + GW // 2].bitcast(BF16))
        by_tile = [stage[:, (5 + 2 * q) * TH:(7 + 2 * q) * TH].rearrange("p (i t h) -> p i t h", i=2, h=H) for q in range(2)]
        flat_sel = sel[:, :, :].rearrange("p a b -> p (a b)")
        tile_mask = [flat_sel[:, q * UG * TILES:(q + 1) * UG * TILES].rearrange("p (i t) -> p i t", t=TILES) for q in range(2)]

        wait(G, *stored_u, marks["flags"])
        k_ue = {}
        for i in range(PG * UG):
            k_ue[i // RS] = c_ue[i // RS].after(G.indirect_dma_start(
                out=ue[:, i, :], out_offset=None, in_=score_table[:, :],
                in_offset=bass.IndirectOffsetOnAxis(ap=src_t[:, i:i + 1], axis=0)), 16)

        wait(V, marks["z3", TILES - 1], *stored)
        wait(A, *stored)
        wait(P, parts_ready, free["bankT", 0], free["bankT", 1], free["bankZ", 0], free["bankZ", 1])
        wait(S, marks["h3T", TILES - 1])
        tb = {}

        def load_places(kind, k):
            counts, table_ap, buffers = (c_dp, dst_places, dp) if kind == "d" else (c_sp, src_places, sp)
            wait(S, tb.get((kind + "hot", k - 2)))
            tb[kind + "rows", k] = counts[k % 2].after(S.dma_start(
                buffers[k % 2], table_ap[k * UG:(k + 1) * UG, :].rearrange("(a i) e -> a (i e)", a=1).to_broadcast([TN, GW])), 16)

        def place_hot(kind, k):
            buffers, hots, column = (dp, dp_hot, 0) if kind == "d" else (sp, sp_hot, 1)
            wait(V, tb[kind + "rows", k], tb.get((kind + "read", k - 3)))
            tb[kind + "hot", k] = c_v.after(V.tensor_scalar(out=hots[k % 3], in0=buffers[k % 2], scalar1=place[0:TN, column:column + 1],
                                                            scalar2=None, op0=ALU.is_equal))

        def target_steps(i0, i1):
            for i in range(i0, min(i1, STEPS)):
                c = i // TC
                if i % UG == 0 and i // UG + 1 < NG:
                    place_hot("d", i // UG + 1)
                    if i // UG + 3 < NG:
                        load_places("d", i // UG + 3)
                if i % TC == 0 and c >= 2:
                    target_sum(c - 2)
                wait(P, tb["dhot", i // UG], tb.get(("te", c - 2)))
                t = step_tile(P, "p", i)
                m = c_p.after(P.matmul(bank[c % 2][:, i % TC * 3 * H:(i % TC + 1) * 3 * H],
                                       dp_hot[i // UG % 3][:, i % UG * CE:(i % UG + 1) * CE],
                                       t3[:, bass.ds(t, 1), :, :].rearrange("p a s h -> p (a s h)"), start=True, stop=True))
                if i % UG == UG - 1:
                    tb["dread", i // UG] = m
                if i % TC == TC - 1:
                    tb["tm", c] = m
            if i1 >= STEPS > i0:
                target_sum(STEPS // TC - 2)
                target_sum(STEPS // TC - 1)

        def target_sum(c):
            wait(V, tb["tm", c])
            tb["te", c] = c_v.after(V.tensor_reduce(te[:, c * TC:(c + 1) * TC, :],
                                                    bank[c % 2][:, 0:TC * 3 * H].rearrange("p (i s h) -> p i h s", s=3, h=H),
                                                    axis=AX.X, op=ALU.add))

        def source_mask(k):
            tile_of = src_tile[:, k * UG:(k + 1) * UG]
            wait(V, tb.get(("keep", k - 2)))
            tb["mask", k] = c_v.after(V.tensor_tensor(tile_mask[k % 2], node_iota[:, None, 0:TILES].to_broadcast([CE, UG, TILES]),
                                                      tile_of[:, :, None].to_broadcast([CE, UG, TILES]), ALU.is_equal))

        def source_product(n):
            k = n // (UG // 2)
            wait(P, tb["shot", k], tb.get(("kept", n - 4)))
            for i in range(2):
                j = 2 * (n % (UG // 2)) + i
                for part in range(3):
                    last = P.matmul(bank[2 + n % 4][:, i * TH:(i + 1) * TH], sp_hot[k % 3][:, j * CE:(j + 1) * CE],
                                    u3[:, part, :, :].rearrange("p t h -> p (t h)"), start=(part == 0), stop=(part == 2))
            tb["sread", k] = tb["sm", n] = c_p.after(last)

        def source_keep(n):
            k, pair = n // (UG // 2), n % (UG // 2)
            wait(V, tb["sm", n], tb["mask", k], tb.get(("summed", n - 2)))
            tb["keep", k] = tb["kept", n] = c_v.after(V.tensor_tensor(
                by_tile[n % 2], bank[2 + n % 4][:, 0:2 * TH].rearrange("p (i t h) -> p i t h", i=2, h=H),
                tile_mask[k % 2][:, 2 * pair:2 * pair + 2, :, None].to_broadcast([CE, 2, TILES, H]), ALU.mult))

        def source_sum(n):
            wait(V, tb["kept", n])
            i0 = PG * UG + 2 * n
            tb["summed", n] = c_v.after(V.tensor_reduce(ue[:, i0:i0 + 2, :], by_tile[n % 2].rearrange("p i t h -> p i h t"),
                                                        axis=AX.X, op=ALU.add))

        def te_done(b):
            return tb["te", -(-(b + 1) * RS // TC) - 1]

        def ue_done(b):
            pairs = ((b + 1) * RS - PG * UG) // 2
            return tb["summed", pairs - 1] if pairs > 0 else None

        def edge_scores(b, half):
            h0 = half * 4
            bk = bank[6 + half]
            wait(P, k_ue.get(b), te_done(b), ue_done(b), tb.get(("z", half)))
            for j in range(4):
                P.matmul(bk[0:RS, j * CE:(j + 1) * CE], ue[:, b * RS:(b + 1) * RS, h0 + j], ident[:, :], start=True, stop=False)
                last = P.matmul(bk[0:RS, j * CE:(j + 1) * CE], te[:, b * RS:(b + 1) * RS, h0 + j], ident[:, :], start=False, stop=True)
            m = c_p.after(last)
            z = zr[:, b, h0:h0 + 4, :]
            zf = z.rearrange("p h e -> p (h e)")
            wait(A, m)
            m = tb["z", half] = c_a.after(A.copy(zf, bk[0:RS, :]))
            wait(V, m)
            m = c_v.after(V.scalar_tensor_tensor(out=zf, in0=zf, scalar=SLOPE, in1=zf, op0=ALU.mult, op1=ALU.max))
            wait(V, m)
            m = c_v.after(V.tensor_tensor(z, z, masked[:, b, None, :].to_broadcast([RS, 4, CE]), ALU.add))
            f = fr[:, b, h0:h0 + 4, :].rearrange("p h e -> p (h e)")
            wait(V, m, flagged[b, 0], flagged[b, 1])
            c_v.after(V.tensor_tensor_scan(f, repeated(b, 0).bitcast(F32), zf, -BIG, ALU.add, ALU.max))
            m = c_v.after(V.tensor_tensor_scan(backwards[:, ::-1], repeated(b, 1).bitcast(F32)[:, ::-1], zf[:, ::-1], -BIG, ALU.add, ALU.max))
            wait(V, m)
            tb["fr", b] = c_v.after(V.tensor_tensor(f, f, backwards, ALU.max))

        for kind in "ds":
            for k in range(2):
                load_places(kind, k)
        place_hot("d", 0)
        place_hot("s", 0)
        load_places("d", 2)
        load_places("s", 2)
        for to, flags, end in ((cont, keep, 0), (cont_back, nlast, CE - 1)):
            m = c_v.after(V.tensor_scalar(out=to, in0=flags, scalar1=-1.0, scalar2=2.0 * BIG, op0=ALU.add, op1=ALU.mult))
            wait(V, m)
            m = c_v.after(V.memset(to[:, :, end:end + 1], -2.0 * BIG))
        for flags in (pf, pb_):
            c_v.after(V.tensor_scalar(out=flags, in0=flags, scalar1=-1.0, scalar2=BIG, op0=ALU.add, op1=ALU.mult))
        flagged = {}

        def repeated(b, back):
            return (wh, wl)[b // 2][0:RS, b % 2 * 2 + back, :]

        wait(A, m, marks["z3", TILES - 1])
        for b in range(RB):
            for back, flags in enumerate((cont, cont_back)):
                flagged[b, back] = c_a.after(A.copy(repeated(b, back).rearrange("p (h e) -> p h e", e=CE),
                                                    flags[:, b, None, :].to_broadcast([RS, H // 2, CE])))

        NSG = NG - PG
        PAIRS = UG // 2
        assert NSG * PAIRS * TP >= STEPS
        for k in range(NSG + 1):
            if k + 1 < NSG:
                place_hot("s", k + 1)
                if k + 3 < NSG:
                    load_places("s", k + 3)
            if k < NSG:
                source_mask(k)
            for pair in range(PAIRS):
                n = k * PAIRS + pair
                if k:
                    source_keep(n - PAIRS)
                    if n > PAIRS:
                        source_sum(n - PAIRS - 1)
                if k < NSG:
                    source_product(n)
                    target_steps(n * TP, (n + 1) * TP)
            if k in SCORES_AFTER:
                edge_scores(SCORES_AFTER[k], 0)
                edge_scores(SCORES_AFTER[k], 1)
        source_sum(NSG * PAIRS - 1)
        for half in range(2):
            edge_scores(RB - 1, half)

        ends = [row8[:, 0, 0:STEPS], row8[:, 1, 0:STEPS]]
        stops = [row8[:, 2, 0:STEPS], row8[:, 3, 0:STEPS]]
        carried = [r8x, flat_ring[0:H, 8 * FW:8 * FW + STEPS]]
        wait(V, tb["fr", RB - 1], tb["sread", NSG - 1])
        c_v.after(V.tensor_copy(edge8[:, :, 0, :], fr[:, :, :, CE - 1]))
        m = c_v.after(V.tensor_copy(edge8[:, :, 1, :], fr[:, :, :, 0]))
        for lane in range(2):
            c_v.after(V.tensor_scalar(out=stops[lane], in0=flags8[:, lane, :], scalar1=-1.0, scalar2=BIG, op0=ALU.add, op1=ALU.mult))
        c_v.after(V.memset(carried[0][:, 0:1], -BIG))
        c_v.after(V.memset(carried[1][:, STEPS - 1:STEPS], -BIG))
        wait(P, m)
        for lane in range(2):
            for b in range(RB):
                last = P.transpose(bank[lane][0:H, b * RS:(b + 1) * RS], edge8[:, b, lane, :], ident[0:RS, 0:RS])
            m = c_p.after(last)
            wait(V, m)
            tb["ends", lane] = c_v.after(V.tensor_copy(ends[lane], bank[lane][0:H, 0:STEPS]))
        wait(V, tb["ends", 1])
        forward = c_v.after(V.tensor_tensor_scan(carried[0][:, 1:STEPS], stops[0][:, 0:STEPS - 1], ends[0][:, 0:STEPS - 1],
                                                 -BIG, ALU.add, ALU.max))
        backward = c_v.after(V.tensor_tensor_scan(carried[1][:, 0:STEPS - 1][:, ::-1], stops[1][:, 1:STEPS][:, ::-1],
                                                  ends[1][:, 1:STEPS][:, ::-1], -BIG, ALU.add, ALU.max))
        for lane, ready in enumerate((forward, backward)):
            wait(P, ready)
            for b in range(RB):
                last = P.transpose(bank[2 + lane][0:RS, b * H:(b + 1) * H], carried[lane][:, b * RS:(b + 1) * RS], ident[0:H, 0:H])
            m = c_p.after(last)
            wait(V, m)
            m = c_v.after(V.tensor_copy(back8[:, :, lane, :], bank[2 + lane][0:RS, 0:RB * H].rearrange("p (b h) -> p b h", b=RB)))

        def clear(tiles, ready):
            wait(G, ready)
            for t in tiles:
                tb["cleared"] = c_g.after(G.memset(acc[0:TN, t, :], 0.0))

        BT = H * CE // D
        clear(range(2 * RB * BT, TILES), forward)
        exps = ue
        for b in range(RB):
            for lane, flags in enumerate((pf, pb_)):
                wait(V, m)
                for h in range(H):
                    m = c_v.after(V.scalar_tensor_tensor(out=fr[:, b, h, :], in0=flags[:, b, :], scalar=back8[:, b, lane, h:h + 1],
                                                         in1=fr[:, b, h, :], op0=ALU.add, op1=ALU.max))
            wait(V, m)
            m = c_v.after(V.tensor_tensor(ex[:, b, :, :], zr[:, b, :, :], fr[:, b, :, :], ALU.subtract))
            clear([n * BT + k for n in (b, RB + b) for k in range(BT)], m)
            wait(A, m)
            m = c_a.after(A.activation(ex[:, b, :, :], ex[:, b, :, :], ACT.Exp))
            for half in range(2):
                wait(P, m, tb.get(("al", half)))
                for j in range(4):
                    last = P.transpose(bank[6 + half][:, j * RS:(j + 1) * RS], ex[:, b, half * 4 + j, :], ident[0:RS, 0:RS])
                mm = c_p.after(last)
                wait(A, mm)
                tb["al", half] = c_a.after(A.copy(exps[:, b * RS:(b + 1) * RS, half * 4:half * 4 + 4].rearrange("p i h -> p h i"),
                                                  bank[6 + half][:, 0:4 * RS].rearrange("p (h i) -> p h i", h=4)))
        wait(V, tb["al", 0], tb["al", 1], tb["cleared"])
        wait(P, tb["al", 0], tb["al", 1])
        wait(A, tb["al", 0], tb["al", 1])
        wait(G, mm, *stored)

        denominators = bank[5][0:TN, 0:TH].rearrange("p (t h) -> p t h", h=H)
        P.matmul(bank[5][0:TN, 0:TH], zero[:, 0:TN], dstf[:, :, :].rearrange("p b e -> p (b e)")[:, 0:TH], start=True, stop=False)

        def add_denominators(i, sel_i):
            t = step_tile(P, "p", i)
            return P.matmul(denominators[:, bass.ds(t, 1), :].rearrange("p a h -> p (a h)"), sel_i, exps[:, i, :],
                            start=False, stop=(i == STEPS - 1))

        k_acc = aggregate(3, acc, False, [], [], alpha=exps, also=add_denominators)

        rden = stage[0:TN, 0:TH].rearrange("p (t h) -> p t h", h=H)
        wait(V, done["pe"][-1])
        m = c_v.after(V.tensor_scalar(out=rden, in0=denominators, scalar1=0.5, scalar2=None, op0=ALU.max))
        wait(V, m)
        m = c_v.after(V.reciprocal(rden, rden))
        wait(V, m)
        wait(A, m)
        wait(G, m)
        for q in range(5):
            by_act = []
            for n in range(XQ):
                t = q * XQ + n
                heads = acc[0:TN, t, :].rearrange("p (h j) -> p h j", h=H)
                x_heads = x[0:TN, t, :].rearrange("p (h j) -> p h j", h=H)
                if n == 0 or (n == XQ - 1 and q in (0, 2)):
                    m = c_g.after(G.tensor_tensor(heads, heads, rden[:, t, :, None].to_broadcast([TN, H, DP]), ALU.mult))
                    wait(G, m)
                    tb["final", t] = c_g.after(G.tensor_tensor(x[0:TN, t, :], x[0:TN, t, :], acc[0:TN, t, :], ALU.add))
                elif n in (1, XQ - 1):
                    for h in range(H):
                        last = A.activation(heads[:, h, :], heads[:, h, :], ACT.Copy, scale=rden[:, t, h:h + 1])
                    by_act.append((t, c_a.after(last)))
                else:
                    for h in range(H):
                        last = V.scalar_tensor_tensor(out=x_heads[:, h, :], in0=heads[:, h, :], scalar=rden[:, t, h:h + 1],
                                                      in1=x_heads[:, h, :], op0=ALU.mult, op1=ALU.add)
                    tb["final", t] = c_v.after(last)
            for t, m in by_act:
                wait(V, m)
                tb["final", t] = c_v.after(V.tensor_tensor(x[0:TN, t, :], x[0:TN, t, :], acc[0:TN, t, :], ALU.add))
            wait(S, *(tb["final", q * XQ + n] for n in range(XQ)))
            c_out[q].after(S.dma_start(out[q * XQ * TN:(q + 1) * XQ * TN, :].rearrange("(t p) d -> p t d", p=TN),
                                       x[0:TN, q * XQ:(q + 1) * XQ, :]), 16)
        for q in range(5):
            wait(S, (c_out[q].sem, c_out[q].value))


INPUTS = ["x", "src", "dst", "edge_weight", "L0_gnn_W", "L1_gnn_W", "L1_gnn_b", "L2_gnn_W1", "L2_gnn_b1",
          "L2_gnn_W2", "L2_gnn_b2", "L3_gnn_Ws", "L3_gnn_Wb", "L3_gnn_a_w", "L3_gnn_a_b"]


def kernel(**inputs):
    import concourse.bacc as bacc
    from concourse.bass_utils import run_bass_kernel_spmd as run

    nc = bacc.Bacc("TRN2", target_bir_lowering=False, num_devices=1)
    arrays, args = {}, []
    for name in INPUTS:
        a = np.ascontiguousarray(inputs[name])
        arrays["in_" + name] = a
        args.append(nc.dram_tensor("in_" + name, a.shape, mybir.dt.from_np(a.dtype), kind="ExternalInput").ap())
    result = nc.dram_tensor("out_0", inputs["x"].shape, F32, kind="ExternalOutput").ap()
    build(nc, *args, result)
    r = run(nc, [arrays], core_ids=[0])
    return r.results[0]["out_0"]
```
